# Optimizing a Trainium2 kernel written in Bass

```python
import numpy as np
import jax
import jax.numpy as jnp

def _softmax(x, axis=-1):
    return jax.nn.softmax(x, axis=axis)

def _gelu(x):
    return jax.nn.gelu(x, approximate=True)

def _silu(x):
    return jax.nn.silu(x)

def _sigmoid(x):
    return jax.nn.sigmoid(x)

def _layernorm(x, axis=-1, eps=1e-05):
    m = jnp.mean(x, axis=axis, keepdims=True)
    v = jnp.var(x, axis=axis, keepdims=True)
    return (x - m) / jnp.sqrt(v + eps)

def _scatter_add(tgt, idx, src, axis=0):
    return tgt.at[idx].add(src)

def _segment_sum(src, seg, n):
    return jax.ops.segment_sum(src, seg, n)
kernel_name = 'mk_gnn_preln_d1_gnn_r32_ac0c36'

def setup_inputs(seed: int=0):
    np.random.seed(seed)
    _w = jnp.asarray

    def _rec_inputs():
        import jax
        import jax.numpy as jnp
        _gk = jax.random.key(seed)
        x = -0.000202 + 1 * jax.random.normal(jax.random.fold_in(_gk, 1), (50000, 128), jnp.float32)
        src = jax.random.randint(jax.random.fold_in(_gk, 2), (50000,), 0, 50000, jnp.int32)
        dst = jax.random.randint(jax.random.fold_in(_gk, 3), (50000,), 0, 50000, jnp.int32)
        _o = jnp.argsort(dst, stable=True)
        src = src[_o]
        dst = dst[_o]
        edge_attr_128 = 5.93493e-05 + 1.00006 * jax.random.normal(jax.random.fold_in(_gk, 11), (50000, 128), jnp.float32)
        return (x, src, dst, edge_attr_128)
    x, src, dst, edge_attr_128 = _rec_inputs()

    def _L0_gnn_setup():
        import jax, jax.numpy as jnp
        import numpy as np
        N_NODES = 50000
        N_EDGES = 18750
        D_NODE = 128
        D_EDGE = 128
        HIDDEN = 128
        LN_EPS = 1e-05

        def _layer_norm(h, gamma, beta):
            mu = jnp.mean(h, axis=-1, keepdims=True)
            var = jnp.mean(jnp.square(h - mu), axis=-1, keepdims=True)
            return (h - mu) * jax.lax.rsqrt(var + LN_EPS) * gamma + beta
        key = jax.random.key(seed)
        ks = jax.random.split(key, 12)
        x = jax.random.normal(ks[0], (N_NODES, D_NODE), dtype=jnp.float32)
        edge_index = jax.random.randint(ks[1], (2, N_EDGES), 0, N_NODES, dtype=jnp.int64)
        edge_attr = jax.random.normal(ks[2], (N_EDGES, D_EDGE), dtype=jnp.float32)
        in_dim = D_NODE + D_EDGE
        s1 = 1.0 / np.sqrt(in_dim)
        s2 = 1.0 / np.sqrt(HIDDEN)
        W1 = jax.random.uniform(ks[3], (in_dim, HIDDEN), minval=-s1, maxval=s1, dtype=jnp.float32)
        b1 = jax.random.uniform(ks[4], (HIDDEN,), minval=-s1, maxval=s1, dtype=jnp.float32)
        W2 = jax.random.uniform(ks[5], (HIDDEN, HIDDEN), minval=-s2, maxval=s2, dtype=jnp.float32)
        b2 = jax.random.uniform(ks[6], (HIDDEN,), minval=-s2, maxval=s2, dtype=jnp.float32)
        W3 = jax.random.uniform(ks[7], (HIDDEN, D_NODE), minval=-s2, maxval=s2, dtype=jnp.float32)
        b3 = jax.random.uniform(ks[8], (D_NODE,), minval=-s2, maxval=s2, dtype=jnp.float32)
        ln_gamma = jnp.ones((D_NODE,), dtype=jnp.float32)
        ln_beta = jnp.zeros((D_NODE,), dtype=jnp.float32)
        return {'x': x, 'edge_index': edge_index, 'edge_attr': edge_attr, 'W1': W1, 'b1': b1, 'W2': W2, 'b2': b2, 'W3': W3, 'b3': b3, 'ln_gamma': ln_gamma, 'ln_beta': ln_beta}
    _L0_gnn_all = _L0_gnn_setup()
    _L0_gnn_in = {k: v for k, v in _L0_gnn_all.items() if k in ('W1', 'b1', 'W2', 'b2', 'W3', 'b3', 'ln_gamma', 'ln_beta')}
    del _L0_gnn_all
    return {'x': x, 'src': src, 'dst': dst, 'edge_attr_128': edge_attr_128, 'L0_gnn_W1': _L0_gnn_in['W1'], 'L0_gnn_b1': _L0_gnn_in['b1'], 'L0_gnn_W2': _L0_gnn_in['W2'], 'L0_gnn_b2': _L0_gnn_in['b2'], 'L0_gnn_W3': _L0_gnn_in['W3'], 'L0_gnn_b3': _L0_gnn_in['b3'], 'L0_gnn_ln_gamma': _L0_gnn_in['ln_gamma'], 'L0_gnn_ln_beta': _L0_gnn_in['ln_beta']}

def reference(x, src, dst, edge_attr_128, L0_gnn_W1, L0_gnn_b1, L0_gnn_W2, L0_gnn_b2, L0_gnn_W3, L0_gnn_b3, L0_gnn_ln_gamma, L0_gnn_ln_beta):
    import jax
    import jax.numpy as jnp

    def _L0_gnn_ref(x, edge_index, edge_attr, W1, b1, W2, b2, W3, b3, ln_gamma, ln_beta):
        import jax, jax.numpy as jnp
        import numpy as np
        N_NODES = 50000
        N_EDGES = 18750
        D_NODE = 128
        D_EDGE = 128
        HIDDEN = 128
        LN_EPS = 1e-05

        def _layer_norm(h, gamma, beta):
            mu = jnp.mean(h, axis=-1, keepdims=True)
            var = jnp.mean(jnp.square(h - mu), axis=-1, keepdims=True)
            return (h - mu) * jax.lax.rsqrt(var + LN_EPS) * gamma + beta
        agg = jax.ops.segment_sum(edge_attr, edge_index[1], num_segments=N_NODES)
        h = jnp.concatenate([x, agg], axis=-1)
        h = jax.nn.relu(h @ W1 + b1)
        h = jax.nn.relu(h @ W2 + b2)
        h = h @ W3 + b3
        return _layer_norm(h, ln_gamma, ln_beta)
    edge_index = jnp.stack([src, dst])
    h = jnp.maximum(_layernorm(x, axis=-1), 0.0)
    x = x + _L0_gnn_ref(h, edge_index, edge_attr_128, L0_gnn_W1, L0_gnn_b1, L0_gnn_W2, L0_gnn_b2, L0_gnn_W3, L0_gnn_b3, L0_gnn_ln_gamma, L0_gnn_ln_beta)
    return x

_drawn_inputs = setup_inputs


def setup_inputs(seed=0):
    import zlib

    import numpy as np

    out = dict(_drawn_inputs(seed))
    spreads = {'L0_gnn_ln_gamma': (1.0, 0.2), 'L0_gnn_ln_beta': (0.0, 0.1)}
    factors = {}
    for name, (base, spread) in spreads.items():
        noise = np.random.default_rng([zlib.crc32(name.encode()), seed]).standard_normal(out[name].shape)
        drawn = base * np.exp(spread * noise) if base else spread * noise
        out[name] = jnp.asarray(drawn.astype(out[name].dtype))
    for name, factor in factors.items():
        out[name] = (out[name] * factor).astype(out[name].dtype)
    return out
```

```python
from contextlib import ExitStack

import concourse.bass as bass
from concourse import mybir

P = 128
ALU = mybir.AluOpType
ACT = mybir.ActivationFunctionType
AX_X = mybir.AxisListType.X
F32 = mybir.dt.float32
BF16 = mybir.dt.bfloat16
I32 = mybir.dt.int32

ROWS = 4
GROUP = P * ROWS
WIN_NODES = 64
WINS = GROUP // WIN_NODES
BLOCK = 16
EPS = 1e-5

UNROLL = 4
X_BUFS = 4
EDGE_BUFS = 4
OUT_BUFS = 4
PAIR = 2
KEEP = 8
LOOP_FROM = 6
LOAD_X_AHEAD = 6
LOAD_E_AHEAD = 5

GEN_COLS = 10
GEN_EDGE_BUFS = 4


class Turn:

    def __init__(self, g, phase=None, whole=None, general=False):
        self.g, self.phase, self.whole, self.general = g, phase, whole, general

    def ring(self, n):
        return 0 if self.general else self.phase % n

    def round(self, n):
        if self.general:
            return self.g
        return self.whole * (UNROLL // n) + self.phase // n

    def depth(self, n):
        return 1 if self.general else n


def wait_count(eng, sem, value):
    if isinstance(value, int) and value <= 0:
        return
    eng.wait_ge(sem, value)


def gnn_layer(nc, x, dst, edge, w1, b1, w2, b2, w3, b3, gamma, beta, out):
    N, D = x.shape
    E = edge.shape[0]
    assert D == P and N % ROWS == 0 and E % BLOCK == 0
    GROUPS = -(-N // GROUP)
    LAST = GROUPS - 1
    LAST_BASE = N - GROUP
    LAST_SKIP = (LAST * GROUP - LAST_BASE) // ROWS
    DST_PARTS = 125
    RUN = E // DST_PARTS
    RUN_BLOCKS = RUN // BLOCK
    assert E % DST_PARTS == 0 and RUN % BLOCK == 0 and GROUPS <= P
    LAST_BLOCK = (E - P) // BLOCK
    TABLE = LAST_BLOCK + 1
    BOUNDS = WINS + 1
    SPAN = P // BLOCK
    GEN_BATCHES = RUN // GEN_COLS
    assert RUN % GEN_COLS == 0 and GEN_BATCHES % GEN_EDGE_BUFS == 0
    LOOP_TURNS = (LAST - LOAD_X_AHEAD - LOOP_FROM) // UNROLL * UNROLL
    LOOP_TO = LOOP_FROM + LOOP_TURNS

    x_rows = x.rearrange("(q r) f -> q (r f)", r=ROWS)
    out_rows = out.rearrange("(q r) f -> q (r f)", r=ROWS)
    dst_runs = dst.rearrange("(q j) -> q j", j=RUN)
    edge_runs = edge.rearrange("(q j) f -> q (j f)", j=RUN)
    dst_table = nc.dram_tensor("dst_table", [TABLE, P], I32, kind="Internal").ap()

    with ExitStack() as ctx:
        def sb(name, shape, dt=F32):
            return ctx.enter_context(nc.sbuf_tensor(name, shape, dt))

        def ps(name, shape=(P, GROUP), dt=F32):
            return ctx.enter_context(nc.psum_tensor(name, list(shape), dt))

        def sem(name):
            return ctx.enter_context(nc.semaphore(name))

        w1x = sb("w1x", [P, P])
        w1a = sb("w1a", [P, P])
        w2s = sb("w2s", [P, P])
        w3s = sb("w3s", [P, P])
        w3c = sb("w3c", [P, P])
        w3mean = sb("w3mean", [P, 1])
        b1c = sb("b1c", [P, 1])
        b2c = sb("b2c", [P, 1])
        b3r = sb("b3r", [1, P])
        b3mean = sb("b3mean", [1, 1])
        b3c = sb("b3c", [1, P])
        b3left = sb("b3left", [1, P])
        b3parts = sb("b3parts", [1, 3, P], BF16)
        b3rows = sb("b3rows", [3, P], BF16)
        ones_bf = sb("ones_bf", [3, P], BF16)
        gamma_all = sb("gamma_all", [P, P])
        beta_all = sb("beta_all", [P, P])
        eps_col = sb("eps_col", [P, 1])
        ones_col = sb("ones_col", [P, 1])
        run_blocks_col = sb("run_blocks_col", [P, 1])
        ident = sb("ident", [P, P])
        local_node = sb("local_node", [P, ROWS, WIN_NODES // ROWS])

        dst_i = sb("dst_i", [DST_PARTS, RUN], I32)
        dst_f = sb("dst_f", [DST_PARTS, RUN])
        next_i = sb("next_i", [DST_PARTS, 1], I32)
        first_f = sb("first_f", [DST_PARTS, 1])
        next_f = sb("next_f", [DST_PARTS, 1])
        bound_row = sb("bound_row", [DST_PARTS, GROUPS, BOUNDS])
        past_first = sb("past_first", [DST_PARTS, GROUPS, BOUNDS])
        past_next = sb("past_next", [DST_PARTS, GROUPS, BOUNDS])
        run_pick = sb("run_pick", [DST_PARTS, GROUPS, BOUNDS])
        past_block = sb("past_block", [RUN_BLOCKS, GROUPS, BOUNDS])
        start_f = sb("start_f", [1, GROUPS, WINS])
        start_i = sb("start_i", [1, GROUPS, WINS], I32)
        rank_col = sb("rank_col", [GROUPS, BOUNDS])
        block_f = sb("block_f", [GROUPS, WINS])
        block_i = sb("block_i", [GROUPS, WINS], I32)
        base_col = sb("base_col", [GROUPS, 1])
        bound_step = sb("bound_step", [GROUPS, WINS])
        bound_col = sb("bound_col", [GROUPS, WINS])
        span = sb("span", [GROUPS, WINS])
        too_far = sb("too_far", [GROUPS, WINS])
        falls = sb("falls", [DST_PARTS, RUN])
        bad = sb("bad", [P, 2])
        bad_i = sb("bad_i", [1, 1], I32)
        bad_f = sb("bad_f", [1, 1])
        dst_win = sb("dst_win", [GROUPS, WINS, P], I32)
        dst_rel = sb("dst_rel", [GROUPS, WINS, P])
        dst_loc = sb("dst_loc", [P, GROUPS, WINS])

        x_in = sb("x_in", [P, X_BUFS, GROUP])
        x_keep = sb("x_keep", [P, KEEP, GROUP])
        edges = sb("edges", [P, EDGE_BUFS, WINS, P])
        stats = sb("stats", [P, PAIR, ROWS, 6])
        mean_var = sb("mean_var", [P, PAIR, ROWS, 2])
        std1 = sb("std1", [P, PAIR, ROWS])
        rstd1 = sb("rstd1", [P, PAIR, ROWS])
        x_hat = sb("x_hat", [P, PAIR, ROWS, P])
        one_hot = sb("one_hot", [P, PAIR, WINS, WIN_NODES])
        x_t = sb("x_t", [P, PAIR, GROUP])
        agg_t = sb("agg_t", [P, PAIR, GROUP])
        h1 = sb("h1", [P, PAIR, GROUP])
        h2 = sb("h2", [P, PAIR, GROUP])
        squares = sb("squares", [P, ROWS, P])
        sum_sq = sb("sum_sq", [P, PAIR, ROWS])
        std2 = sb("std2", [P, PAIR, ROWS])
        rstd2 = sb("rstd2", [P, PAIR, ROWS])
        result = sb("result", [P, OUT_BUFS, ROWS, P])

        gen_edges = sb("gen_edges", [DST_PARTS, GEN_EDGE_BUFS, GEN_COLS, P])
        gen_hot = sb("gen_hot", [DST_PARTS, PAIR, GEN_COLS, GROUP])
        gen_rel = sb("gen_rel", [DST_PARTS, RUN])
        group_node = sb("group_node", [DST_PARTS, ROWS, P])
        zeros = sb("zeros", [P, GROUP])

        x_ps = [ps(f"x_ps{i}") for i in range(PAIR)]
        agg_ps = [ps(f"agg_ps{i}") for i in range(PAIR)]
        h1_ps = ps("h1_ps")
        h2_ps = ps("h2_ps")
        y_ps = [ps(f"y_ps{i}") for i in range(PAIR)]

        s_dst = sem("dst_loaded")
        s_next = sem("next_loaded")
        s_table = sem("table_written")
        s_weights = sem("weights_loaded")
        s_consts = sem("consts_made")
        s_iota = sem("bounds_made")
        s_ident0 = sem("ident_cleared")
        s_prep = sem("weights_prepared")
        s_b3 = sem("b3_rows_placed")
        s_ix = sem("index_steps")
        s_pick = sem("blocks_picked")
        s_rank = sem("ranks_counted")
        s_win = sem("dst_windows_loaded")
        s_turned = sem("dst_turned")
        s_badsum = sem("bad_summed")

        s_x = [sem(f"x_loaded{i}") for i in range(X_BUFS)]
        s_e = [sem(f"edges_loaded{i}") for i in range(EDGE_BUFS)]
        s_stored = [sem(f"stored{i}") for i in range(OUT_BUFS)]
        s_stats = sem("stats_ready")
        s_var = sem("var_ready")
        s_std1 = sem("std1_ready")
        s_rstd1 = sem("rstd1_ready")
        s_hat = sem("x_hat_ready")
        s_keep = sem("x_keep_ready")
        s_hot = sem("one_hot_ready")
        s_xps = sem("x_ps_ready")
        s_aggps = sem("agg_ps_ready")
        s_xt = sem("x_t_ready")
        s_aggt = sem("agg_t_ready")
        s_h1ps = sem("h1_ps_ready")
        s_h1 = sem("h1_ready")
        s_h2ps = sem("h2_ps_ready")
        s_h2 = sem("h2_ready")
        s_yps = sem("y_ps_ready")
        s_sq = sem("sum_sq_ready")
        s_std2 = sem("std2_ready")
        s_rstd2 = sem("rstd2_ready")
        s_scaled = sem("scaled_ready")
        s_out = sem("out_ready")

        s_ge = [sem(f"gen_edges_loaded{i}") for i in range(GEN_EDGE_BUFS)]
        s_ghot = sem("gen_hot_ready")
        s_gmm = sem("gen_batches_summed")
        s_grel = sem("gen_rel_steps")

        WEIGHT_LOADS = 9
        HALF = GROUPS // 2
        assert GROUPS % 2 == 0 and HALF * BOUNDS <= 512

        def all_turns(eng, turn):
            for i in range(-LOAD_X_AHEAD, LOOP_FROM):
                turn(lambda ahead, i=i: Turn(i + ahead, i + ahead, 0))
            with eng.Fori(0, LOOP_TURNS // UNROLL) as j:
                first = eng.snap(j * UNROLL)
                for u in range(UNROLL):
                    phase = LOOP_FROM + u
                    turn(lambda ahead, u=u, phase=phase: Turn(first + (phase + ahead), phase + ahead, j))
            for i in range(LOOP_TO, GROUPS + 4):
                turn(lambda ahead, i=i: Turn(i + ahead, i + ahead, 0))

        def there(t):
            return not isinstance(t.g, int) or 0 <= t.g < GROUPS

        def is_last(t):
            return isinstance(t.g, int) and t.g == LAST

        def two_paths(eng, fast, general):
            eng.wait_ge(s_ix, IX_DONE)
            flag = eng.value_load(bad_i[0:1, 0:1], min_val=0, max_val=2 * P)
            with eng.If(flag < 1):
                fast()
            with eng.Else():
                general()

        def general_turns(eng, turn):
            with eng.Fori(0, LAST) as g:
                turn(Turn(g, general=True))
            turn(Turn(LAST, general=True))

        IX_DONE = 16
        PREPARED = 12

        block = ctx.enter_context(nc.Block())

        @block.sync
        def _(sp):
            sp.dma_start(dst_i[:, :], dst_runs).then_inc(s_dst, 16)
            with nc.allow_non_contiguous_dma("one first dst of each run"):
                sp.dma_start(next_i[0:DST_PARTS - 1, :], dst_runs[1:DST_PARTS, 0:1]).then_inc(s_next, 16)
            rows = TABLE // 16 * 16
            for r0, r1 in ((0, rows), (rows, TABLE)):
                src = bass.AP(dst.tensor, BLOCK * r0, [[BLOCK, r1 - r0], [1, P]])
                sp.dma_start(dst_table[r0:r1, :], src).then_inc(s_table, 16)
            for tile, src in ((w1x, w1[0:P, :]), (w1a, w1[P:2 * P, :]), (w2s, w2), (w3s, w3)):
                sp.dma_start(tile[:, :], src).then_inc(s_weights, 16)
            with nc.allow_non_contiguous_dma("a bias is a column"):
                for tile, src in ((b1c, b1), (b2c, b2)):
                    sp.dma_start(tile[:, :], src.rearrange("(p o) -> p o", o=1)).then_inc(s_weights, 16)
            sp.dma_start(b3r[:, :], b3.rearrange("(o f) -> o f", o=1)).then_inc(s_weights, 16)
            for tile, src in ((gamma_all, gamma), (beta_all, beta)):
                sp.dma_start(tile[:, :], bass.AP(src.tensor, 0, [[0, P], [1, P]])).then_inc(s_weights, 16)
            sp.wait_ge(s_prep, 8)
            for k in range(3):
                sp.dma_start(b3rows[k:k + 1, :], b3parts[0:1, k, :]).then_inc(s_b3, 16)

            def load_x(t):
                if not there(t):
                    return
                wait_count(sp, s_hat, t.g - t.depth(X_BUFS) + 1)
                wait_count(sp, s_keep, t.g - t.depth(X_BUFS) + 1)
                row = LAST_BASE // ROWS if is_last(t) else t.g * P
                sp.dma_start(x_in[:, t.ring(X_BUFS), :], x_rows[bass.ds(row, P), :]) \
                    .then_inc(s_x[t.ring(X_BUFS)], 16)

            def load_edges(t):
                if not there(t):
                    return
                wait_count(sp, s_aggps, t.g - EDGE_BUFS + 1)
                _, starts = nc.values_load_multi_w_load_instructions(
                    start_i[0:1, bass.ds(t.g, 1), :].rearrange("o g w -> o (g w)"), engines=[sp.engine],
                    min_val=0, max_val=E - P, skip_runtime_bounds_check_because="the index stage keeps starts within 0 and E - P")
                for w in range(WINS):
                    sp.dma_start(edges[:, t.ring(EDGE_BUFS), w, :], edge[bass.ds(starts[w], P), :]) \
                        .then_inc(s_e[t.ring(EDGE_BUFS)], 16)

            def fast():
                def turn(at):
                    load_x(at(LOAD_X_AHEAD))
                    load_edges(at(LOAD_E_AHEAD))
                all_turns(sp, turn)

            def general():
                def turn(t):
                    load_x(t)
                    with sp.Fori(0, GEN_BATCHES // GEN_EDGE_BUFS) as k:
                        for b in range(GEN_EDGE_BUFS):
                            sp.wait_ge(s_gmm, t.g * GEN_BATCHES + k * GEN_EDGE_BUFS + (b + 1))
                            sp.dma_start(gen_edges[:, b, :, :].rearrange("p c f -> p (c f)"),
                                         edge_runs[:, bass.ds((k * GEN_EDGE_BUFS + b) * GEN_COLS * P, GEN_COLS * P)]) \
                                .then_inc(s_ge[b], 16)
                general_turns(sp, turn)

            two_paths(sp, fast, general)

        @block.gpsimd
        def _(pool):
            pool.iota(bound_row[:, 0:LAST, :], [[GROUP, LAST], [WIN_NODES, BOUNDS]], base=0,
                      channel_multiplier=0, allow_small_or_imprecise_dtypes=True)
            pool.iota(bound_row[:, LAST:GROUPS, :], [[0, 1], [WIN_NODES, BOUNDS]], base=LAST_BASE,
                      channel_multiplier=0, allow_small_or_imprecise_dtypes=True).then_inc(s_iota, 1)
            pool.memset(ident[:, :], 0.0).then_inc(s_ident0, 1)
            pool.wait_ge(s_ident0, 1)
            pool.affine_select(out=ident[:, :], in_=ident[:, :], compare_op=ALU.not_equal, fill=1.0,
                               base=0, pattern=[[-1, P]], channel_multiplier=1)
            pool.iota(base_col[:, :], [[0, 1]], base=0, channel_multiplier=GROUP,
                      allow_small_or_imprecise_dtypes=True)
            pool.iota(bound_step[:, :], [[WIN_NODES, WINS]], base=0, channel_multiplier=0,
                      allow_small_or_imprecise_dtypes=True)
            pool.iota(local_node[:, :, :], [[1, ROWS], [ROWS, WIN_NODES // ROWS]], base=0,
                      channel_multiplier=0, allow_small_or_imprecise_dtypes=True)
            pool.iota(group_node[:, :, :], [[1, ROWS], [ROWS, P]], base=0,
                      channel_multiplier=0, allow_small_or_imprecise_dtypes=True).then_inc(s_consts, 1)
            pool.wait_ge(s_table, 32)
            pool.wait_ge(s_ix, 8)
            for w in range(WINS):
                pool.indirect_dma_start(
                    out=dst_win[:, w, :], out_offset=None, in_=dst_table[:, :],
                    in_offset=bass.IndirectOffsetOnAxis(ap=block_i[:, w:w + 1], axis=0)).then_inc(s_win, 16)
            pool.wait_ge(s_weights, 16 * WEIGHT_LOADS)

            def keep_x(t):
                if not there(t):
                    return
                pool.wait_ge(s_x[t.ring(X_BUFS)], (t.round(X_BUFS) + 1) * 16)
                wait_count(pool, s_out, t.g - t.depth(KEEP) + 1)
                pool.tensor_tensor(kept(t), x_in[:, t.ring(X_BUFS), :].rearrange("p (r f) -> p r f", r=ROWS),
                                   beta_all[:, :].unsqueeze(1).to_broadcast([P, ROWS, P]), ALU.add) \
                    .then_inc(s_keep, 1)

            def kept(t):
                slot = t.g % KEEP if isinstance(t.g, int) else t.g & (KEEP - 1)
                if t.general:
                    slot = 0
                return x_keep[:, bass.ds(slot, 1), :].rearrange("p o (r f) -> p (o r) f", r=ROWS)

            def add_x(t):
                if not there(t):
                    return
                pool.wait_ge(s_scaled, t.g + 1)
                pool.wait_ge(s_keep, t.g + 1)
                r = result[:, t.ring(OUT_BUFS), :, :]
                pool.tensor_tensor(r, r, kept(t), ALU.add).then_inc(s_out, 1)

            def store(t):
                if not there(t):
                    return
                pool.wait_ge(s_out, t.g + 1)
                skip = LAST_SKIP if is_last(t) else 0
                row = LAST_BASE // ROWS + skip if is_last(t) else t.g * P
                pool.dma_start(out_rows[bass.ds(row, P - skip), :],
                               result[skip:P, t.ring(OUT_BUFS), :, :].rearrange("p r f -> p (r f)")) \
                    .then_inc(s_stored[t.ring(OUT_BUFS)], 16)

            def fast():
                def turn(at):
                    keep_x(at(2))
                    add_x(at(-2))
                    store(at(-2))
                all_turns(pool, turn)
                for i in range(OUT_BUFS):
                    pool.wait_ge(s_stored[i], 16 * len(range(i, GROUPS, OUT_BUFS)))

            def general():
                def turn(t):
                    keep_x(t)
                    add_x(t)
                    store(t)
                general_turns(pool, turn)
                pool.wait_ge(s_stored[0], 16 * GROUPS)

            two_paths(pool, fast, general)

        @block.scalar
        def _(act):
            act.wait_ge(s_prep, 8)
            act.wait_ge(s_weights, 16 * WEIGHT_LOADS)

            def std_x(t):
                if not there(t):
                    return
                act.wait_ge(s_var, t.g + 1)
                wait_count(act, s_rstd1, t.g - t.depth(PAIR) + 1)
                act.activation(std1[:, t.ring(PAIR), :], mean_var[:, t.ring(PAIR), :, 1], ACT.Sqrt,
                               bias=eps_col[:, :]).then_inc(s_std1, 1)

            def relu_x(t):
                if not there(t):
                    return
                act.wait_ge(s_xps, t.g + 1)
                wait_count(act, s_h1ps, t.g - t.depth(PAIR) + 1)
                act.activation(x_t[:, t.ring(PAIR), :], x_ps[t.ring(PAIR)][:, :], ACT.Relu).then_inc(s_xt, 1)

            def relu_h1(t):
                if not there(t):
                    return
                act.wait_ge(s_h1ps, t.g + 1)
                wait_count(act, s_h2ps, t.g - t.depth(PAIR) + 1)
                act.activation(h1[:, t.ring(PAIR), :], h1_ps[:, :], ACT.Relu, bias=b1c[:, :]).then_inc(s_h1, 1)

            def relu_h2(t):
                if not there(t):
                    return
                act.wait_ge(s_h2ps, t.g + 1)
                wait_count(act, s_yps, t.g - t.depth(PAIR) + 1)
                act.activation(h2[:, t.ring(PAIR), :], h2_ps[:, :], ACT.Relu, bias=b2c[:, :]).then_inc(s_h2, 1)

            def sum_squares(t):
                if not there(t):
                    return
                act.wait_ge(s_yps, t.g + 1)
                for r in range(ROWS):
                    last = act.activation(squares[:, r, :], y_ps[t.ring(PAIR)][:, r * P:(r + 1) * P], ACT.Square,
                                          accum_out=sum_sq[:, t.ring(PAIR), r:r + 1])
                last.then_inc(s_sq, 1)

            def std_y(t):
                if not there(t):
                    return
                act.wait_ge(s_sq, t.g + 1)
                wait_count(act, s_rstd2, t.g - t.depth(PAIR) + 1)
                act.activation(std2[:, t.ring(PAIR), :], sum_sq[:, t.ring(PAIR), :], ACT.Sqrt,
                               bias=eps_col[:, :], scale=1.0 / D).then_inc(s_std2, 1)

            def fast():
                def turn(at):
                    sum_squares(at(-2))
                    std_y(at(-2))
                    std_x(at(3))
                    relu_h1(at(0))
                    relu_x(at(1))
                    relu_h2(at(0))
                all_turns(act, turn)

            def general():
                def turn(t):
                    for stage in (std_x, relu_x, relu_h1, relu_h2, sum_squares, std_y):
                        stage(t)
                general_turns(act, turn)

            two_paths(act, fast, general)

        @block.vector
        def _(dve):
            steps = [0]

            def step(ins):
                steps[0] += 1
                ins.then_inc(s_ix, 1)
                dve.wait_ge(s_ix, steps[0])

            dve.memset(ones_col[:, :], 1.0)
            dve.memset(run_blocks_col[:, :], float(RUN_BLOCKS))
            dve.memset(bad[:, :], 0.0)
            dve.memset(eps_col[:, :], EPS)
            dve.memset(ones_bf[:, :], 1.0)
            dve.memset(zeros[:, :], 0.0)
            step(dve.memset(next_f[:, :], float(N)))
            dve.wait_ge(s_dst, 16)
            dve.wait_ge(s_next, 16)
            dve.tensor_copy(next_f[0:DST_PARTS - 1, :], next_i[0:DST_PARTS - 1, :])
            dve.tensor_copy(first_f[:, :], dst_i[:, 0:1])
            step(dve.tensor_copy(dst_f[:, :], dst_i[:, :]))
            step(dve.memset(first_f[0:1, :], -1.0))
            dve.wait_ge(s_iota, 1)
            dve.tensor_scalar(past_first[:, :, :], bound_row[:, :, :], first_f[:, 0:1], None, ALU.is_gt)
            step(dve.tensor_scalar(past_next[:, :, :], bound_row[:, :, :], next_f[:, 0:1], None, ALU.is_gt))
            step(dve.tensor_tensor(run_pick[:, :, :], past_first[:, :, :], past_next[:, :, :], ALU.subtract))
            dve.wait_ge(s_pick, 2)
            for half in range(2):
                last = dve.tensor_tensor(
                    past_block[:, half * HALF:(half + 1) * HALF, :],
                    x_ps[half][0:RUN_BLOCKS, 0:HALF * BOUNDS].rearrange("p (g b) -> p g b", b=BOUNDS),
                    bound_row[0:RUN_BLOCKS, half * HALF:(half + 1) * HALF, :], ALU.is_lt)
            step(last)
            assert steps[0] == 6
            dve.wait_ge(s_rank, 1)
            step(dve.tensor_scalar(block_f[:, :], agg_ps[0][0:GROUPS, 0:BOUNDS][:, 0:WINS], -float(RUN_BLOCKS + 1),
                                   0.0, ALU.add, ALU.max))
            step(dve.tensor_scalar(block_i[:, :], block_f[:, :], float(LAST_BLOCK), None, ALU.min))
            assert steps[0] == 8
            dve.wait_ge(s_rank, 2)
            for half in range(2):
                rows = (h1_ps, h2_ps)[half][0:1, 0:HALF * BOUNDS].rearrange("p (g b) -> p g b", b=BOUNDS)
                last = dve.tensor_scalar(start_f[:, half * HALF:(half + 1) * HALF, :], rows[:, :, 0:WINS],
                                         -float(RUN_BLOCKS + 1), 0.0, ALU.add, ALU.max)
            step(last)
            step(dve.tensor_scalar(start_i[:, :, :], start_f[:, :, :], float(LAST_BLOCK), float(BLOCK),
                                   ALU.min, ALU.mult))
            step(dve.tensor_scalar(block_f[:, :], block_f[:, :], float(LAST_BLOCK), None, ALU.min))
            step(dve.tensor_tensor(span[:, :], agg_ps[0][0:GROUPS, 1:BOUNDS], block_f[:, :], ALU.subtract))
            step(dve.tensor_scalar(too_far[:, :], span[:, :], SPAN + RUN_BLOCKS + 0.5, None, ALU.is_gt))
            dve.tensor_reduce(bad[0:GROUPS, 0:1], too_far[:, :], AX_X, ALU.max)
            dve.tensor_tensor(falls[:, RUN - 1:RUN], dst_f[:, RUN - 1:RUN], next_f[:, :], ALU.is_gt)
            step(dve.tensor_tensor(falls[:, 0:RUN - 1], dst_f[:, 0:RUN - 1], dst_f[:, 1:RUN], ALU.is_gt))
            step(dve.tensor_reduce(bad[0:DST_PARTS, 1:2], falls[:, :], AX_X, ALU.max))
            assert steps[0] == 15
            dve.wait_ge(s_badsum, 1)
            dve.tensor_reduce(bad_f[:, :], agg_ps[1][0:1, 0:2], AX_X, ALU.add).then_inc(s_prep, 1)
            dve.wait_ge(s_prep, 1)
            step(dve.tensor_copy(bad_i[:, :], bad_f[:, :]))
            assert steps[0] == IX_DONE

            dve.wait_ge(s_weights, 16 * WEIGHT_LOADS)
            dve.tensor_reduce(b3mean[:, :], b3r[:, :], AX_X, ALU.add)
            dve.tensor_reduce(w3mean[:, :], w3s[:, :], AX_X, ALU.add).then_inc(s_prep, 1)
            dve.wait_ge(s_prep, 2)
            dve.tensor_scalar(b3mean[:, :], b3mean[:, :], 1.0 / D, None, ALU.mult)
            dve.tensor_scalar(w3mean[:, :], w3mean[:, :], 1.0 / D, None, ALU.mult).then_inc(s_prep, 1)
            dve.wait_ge(s_prep, 3)
            dve.tensor_scalar(w3c[:, :], w3s[:, :], w3mean[:, 0:1], None, ALU.subtract)
            dve.tensor_scalar(b3c[:, :], b3r[:, :], b3mean[:, 0:1], None, ALU.subtract).then_inc(s_prep, 1)
            dve.wait_ge(s_prep, 4)
            dve.tensor_copy(b3parts[:, 0, :], b3c[:, :]).then_inc(s_prep, 1)
            dve.wait_ge(s_prep, 5)
            dve.tensor_tensor(b3left[:, :], b3c[:, :], b3parts[:, 0, :], ALU.subtract).then_inc(s_prep, 1)
            dve.wait_ge(s_prep, 6)
            dve.tensor_copy(b3parts[:, 1, :], b3left[:, :]).then_inc(s_prep, 1)
            dve.wait_ge(s_prep, 7)
            dve.tensor_tensor(b3parts[:, 2, :], b3left[:, :], b3parts[:, 1, :], ALU.subtract).then_inc(s_prep, 1)

            dve.wait_ge(s_consts, 1)
            dve.tensor_scalar(base_col[:, :], base_col[:, :], float(LAST_BASE), None, ALU.min).then_inc(s_prep, 1)
            dve.wait_ge(s_prep, 9)
            dve.tensor_scalar(bound_col[:, :], bound_step[:, :], base_col[:, 0:1], None, ALU.add).then_inc(s_prep, 1)
            dve.wait_ge(s_prep, 10)
            dve.wait_ge(s_win, 16 * WINS)
            dve.tensor_tensor(dst_rel[:, :, :], dst_win[:, :, :],
                              bound_col[:, :].unsqueeze(2).to_broadcast([GROUPS, WINS, P]),
                              ALU.subtract).then_inc(s_prep, 1)
            dve.wait_ge(s_turned, 1)
            for half in range(2):
                last = dve.tensor_copy(
                    dst_loc[:, :, half * 4:half * 4 + 4].rearrange("p g w -> p w g"),
                    y_ps[half][:, 0:4 * GROUPS].rearrange("p (w g) -> p w g", w=4))
            last.then_inc(s_prep, 1)
            dve.wait_ge(s_prep, PREPARED)

            def x_rows_of(t):
                return x_in[:, t.ring(X_BUFS), :].rearrange("p (r f) -> p r f", r=ROWS)

            def x_stats(t):
                if not there(t):
                    return
                dve.wait_ge(s_x[t.ring(X_BUFS)], (t.round(X_BUFS) + 1) * 16)
                for r in range(ROWS):
                    last = dve.bn_stats(stats[:, t.ring(PAIR), r, :], x_rows_of(t)[:, r, :])
                last.then_inc(s_stats, 1)
                dve.wait_ge(s_stats, t.g + 1)

            def x_mean_var(t):
                if not there(t):
                    return
                for r in range(ROWS):
                    last = dve.bn_aggr(mean_var[:, t.ring(PAIR), r, :], stats[:, t.ring(PAIR), r, :])
                last.then_inc(s_var, 1)

            def normalise(t):
                if not there(t):
                    return
                dve.wait_ge(s_std1, t.g + 1)
                dve.reciprocal(rstd1[:, t.ring(PAIR), :], std1[:, t.ring(PAIR), :]).then_inc(s_rstd1, 1)
                dve.wait_ge(s_rstd1, t.g + 1)
                wait_count(dve, s_xps, t.g - t.depth(PAIR) + 1)
                for r in range(ROWS):
                    last = dve.tensor_scalar(x_hat[:, t.ring(PAIR), r, :], x_rows_of(t)[:, r, :],
                                             mean_var[:, t.ring(PAIR), r, 0:1], rstd1[:, t.ring(PAIR), r:r + 1],
                                             ALU.subtract, ALU.mult)
                last.then_inc(s_hat, 1)

            def make_one_hot(t):
                if not there(t):
                    return
                wait_count(dve, s_aggps, t.g - PAIR + 1)
                dve.tensor_tensor(
                    one_hot[:, t.ring(PAIR), :, :],
                    local_node[:, :, :].rearrange("p r c -> p (r c)").unsqueeze(1).to_broadcast([P, WINS, WIN_NODES]),
                    dst_loc[:, bass.ds(t.g, 1), :].rearrange("p o w -> p (o w)").unsqueeze(2)
                    .to_broadcast([P, WINS, WIN_NODES]), ALU.is_equal).then_inc(s_hot, 1)

            def copy_agg(t):
                if not there(t):
                    return
                dve.wait_ge(s_aggps, t.g + 1)
                wait_count(dve, s_h1ps, t.g - t.depth(PAIR) + 1)
                dve.tensor_copy(agg_t[:, t.ring(PAIR), :], agg_ps[t.ring(PAIR)][:, :]).then_inc(s_aggt, 1)

            def scale_y(t):
                if not there(t):
                    return
                dve.wait_ge(s_std2, t.g + 1)
                dve.reciprocal(rstd2[:, t.ring(PAIR), :], std2[:, t.ring(PAIR), :]).then_inc(s_rstd2, 1)
                dve.wait_ge(s_rstd2, t.g + 1)
                wait_count(dve, s_stored[t.ring(OUT_BUFS)], t.round(OUT_BUFS) * 16)
                for r in range(ROWS):
                    last = dve.scalar_tensor_tensor(
                        out=result[:, t.ring(OUT_BUFS), r, :], in0=y_ps[t.ring(PAIR)][:, r * P:(r + 1) * P],
                        scalar=rstd2[:, t.ring(PAIR), r:r + 1], in1=gamma_all[:, :], op0=ALU.mult, op1=ALU.mult)
                last.then_inc(s_scaled, 1)

            def fast():
                def turn(at):
                    x_stats(at(3))
                    scale_y(at(-2))
                    x_mean_var(at(3))
                    copy_agg(at(1))
                    normalise(at(2))
                    make_one_hot(at(2))
                all_turns(dve, turn)

            def general():
                dve.tensor_copy(gen_rel[:, :], dst_f[:, :]).then_inc(s_grel, 1)

                def turn(t):
                    x_stats(t)
                    dve.memset(bad_f[:, :], 0.0)
                    x_mean_var(t)
                    normalise(t)
                    dve.wait_ge(s_prep, PREPARED)
                    dve.wait_ge(s_grel, t.g + 1)
                    if is_last(t):
                        dve.tensor_scalar(gen_rel[:, :], gen_rel[:, :], float(LAST * GROUP - LAST_BASE), None,
                                          ALU.add).then_inc(s_grel, 1)
                        dve.wait_ge(s_grel, LAST + 2)
                    with dve.Fori(0, GEN_BATCHES // PAIR) as k:
                        for b in range(PAIR):
                            dve.wait_ge(s_gmm, t.g * GEN_BATCHES + k * PAIR + (b + GEN_EDGE_BUFS - PAIR + 1))
                            for c in range(GEN_COLS):
                                last = dve.tensor_scalar(
                                    gen_hot[:, b, c, :], group_node[:, :, :].rearrange("p r c -> p (r c)"),
                                    gen_rel[:, bass.ds((k * PAIR + b) * GEN_COLS + c, 1)], None, ALU.is_equal)
                            last.then_inc(s_ghot, 1)
                    if not is_last(t):
                        dve.wait_ge(s_ghot, (t.g + 1) * GEN_BATCHES)
                        dve.tensor_scalar(gen_rel[:, :], gen_rel[:, :], -float(GROUP), None,
                                          ALU.add).then_inc(s_grel, 1)
                    copy_agg(t)
                    scale_y(t)
                general_turns(dve, turn)

            two_paths(dve, fast, general)

        @block.tensor
        def _(pe):
            pe.wait_ge(s_ix, 5)
            for half in range(2):
                pe.matmul(x_ps[half][0:RUN_BLOCKS, 0:HALF * BOUNDS], dst_f[:, 0:RUN:BLOCK],
                          run_pick[:, half * HALF:(half + 1) * HALF, :].rearrange("p g b -> p (g b)"),
                          start=True, stop=True).then_inc(s_pick, 1)
            pe.wait_ge(s_ix, 6)
            for b in range(BOUNDS):
                pe.matmul(agg_ps[0][0:GROUPS, b:b + 1], past_first[:, :, b], run_blocks_col[0:DST_PARTS, :],
                          start=True, stop=False)
                last = pe.matmul(agg_ps[0][0:GROUPS, b:b + 1], past_block[:, :, b], ones_col[0:RUN_BLOCKS, :],
                                 start=False, stop=True)
            last.then_inc(s_rank, 1)
            for half in range(2):
                part = slice(half * HALF, (half + 1) * HALF)
                row = (h1_ps, h2_ps)[half][0:1, 0:HALF * BOUNDS]
                pe.matmul(row, run_blocks_col[0:DST_PARTS, :], past_first[:, part, :].rearrange("p g b -> p (g b)"),
                          start=True, stop=False)
                last = pe.matmul(row, ones_col[0:RUN_BLOCKS, :], past_block[:, part, :].rearrange("p g b -> p (g b)"),
                                 start=False, stop=True)
            last.then_inc(s_rank, 1)
            pe.wait_ge(s_ix, 15)
            pe.matmul(agg_ps[1][0:1, 0:2], ones_col[:, :], bad[:, :], start=True, stop=True).then_inc(s_badsum, 1)
            pe.wait_ge(s_consts, 1)
            pe.wait_ge(s_prep, 11)
            for w in range(WINS):
                last = pe.transpose(y_ps[w // 4][:, (w % 4) * GROUPS:(w % 4 + 1) * GROUPS], dst_rel[:, w, :],
                                    ident[0:GROUPS, 0:GROUPS])
            last.then_inc(s_turned, 1)
            pe.wait_ge(s_prep, PREPARED)
            pe.wait_ge(s_b3, 48)
            pe.wait_ge(s_weights, 16 * WEIGHT_LOADS)

            def turn_x(t):
                if not there(t):
                    return
                pe.wait_ge(s_hat, t.g + 1)
                wait_count(pe, s_xt, t.g - t.depth(PAIR) + 1)
                for r in range(ROWS):
                    last = pe.transpose(x_ps[t.ring(PAIR)][:, r * P:(r + 1) * P], x_hat[:, t.ring(PAIR), r, :],
                                        ident[:, :])
                last.then_inc(s_xps, 1)

            def sum_windows(t):
                if not there(t):
                    return
                pe.wait_ge(s_hot, t.g + 1)
                pe.wait_ge(s_e[t.ring(EDGE_BUFS)], (t.round(EDGE_BUFS) + 1) * (16 * WINS))
                wait_count(pe, s_aggt, t.g - PAIR + 1)
                cols = agg_ps[t.ring(PAIR)][:, :].rearrange("p (r c) -> p r c", r=ROWS)
                n = WIN_NODES // ROWS
                for w in range(WINS):
                    last = pe.matmul(cols[:, :, w * n:(w + 1) * n], edges[:, t.ring(EDGE_BUFS), w, :],
                                     one_hot[:, t.ring(PAIR), w, :].rearrange("p (r c) -> p r c", r=ROWS),
                                     start=True, stop=True)
                last.then_inc(s_aggps, 1)

            def layer1(t):
                if not there(t):
                    return
                pe.wait_ge(s_xt, t.g + 1)
                pe.wait_ge(s_aggt, t.g + 1)
                wait_count(pe, s_h1, t.g)
                pe.matmul(h1_ps[:, :], w1x[:, :], x_t[:, t.ring(PAIR), :], start=True, stop=False)
                pe.matmul(h1_ps[:, :], w1a[:, :], agg_t[:, t.ring(PAIR), :], start=False, stop=True) \
                    .then_inc(s_h1ps, 1)

            def layer2(t):
                if not there(t):
                    return
                pe.wait_ge(s_h1, t.g + 1)
                wait_count(pe, s_h2, t.g)
                pe.matmul(h2_ps[:, :], w2s[:, :], h1[:, t.ring(PAIR), :], start=True, stop=True).then_inc(s_h2ps, 1)

            def layer3(t):
                if not there(t):
                    return
                pe.wait_ge(s_h2, t.g + 1)
                wait_count(pe, s_scaled, t.g - t.depth(PAIR) + 1)
                y = y_ps[t.ring(PAIR)]
                pe.matmul(y[:, :].rearrange("p (r f) -> p r f", r=ROWS), ones_bf[:, :],
                          b3rows[:, :].unsqueeze(1).to_broadcast([3, ROWS, P]), start=True, stop=False,
                          skip_group_check=True)
                for r in range(ROWS):
                    last = pe.matmul(y[:, r * P:(r + 1) * P], h2[:, t.ring(PAIR), r * P:(r + 1) * P], w3c[:, :],
                                     start=False, stop=(r == ROWS - 1), skip_group_check=True)
                last.then_inc(s_yps, 1)

            def fast():
                def turn(at):
                    layer1(at(0))
                    turn_x(at(1))
                    sum_windows(at(1))
                    layer2(at(0))
                    layer3(at(-1))
                all_turns(pe, turn)

            def general():
                pe.sem_inc(s_gmm, GEN_EDGE_BUFS)

                def sum_all(t):
                    wait_count(pe, s_aggt, t.g)
                    pe.matmul(agg_ps[0][:, :], zeros[:, 0:P], zeros[:, :], start=True, stop=False)
                    with pe.Fori(0, GEN_BATCHES // GEN_EDGE_BUFS) as k:
                        for b in range(GEN_EDGE_BUFS):
                            nth = pe.snap(t.g * (GEN_BATCHES // GEN_EDGE_BUFS) + k)
                            pe.wait_ge(s_ge[b], (nth + 1) * 16)
                            pe.wait_ge(s_ghot, nth * GEN_EDGE_BUFS + b + 1)
                            for c in range(GEN_COLS):
                                last = pe.matmul(agg_ps[0][:, :], gen_edges[:, b, c, :], gen_hot[:, b % PAIR, c, :],
                                                 start=False, stop=False, skip_group_check=True)
                            last.then_inc(s_gmm, 1)
                    pe.matmul(agg_ps[0][:, :], zeros[:, 0:P], zeros[:, :], start=False, stop=True,
                              skip_group_check=True).then_inc(s_aggps, 1)

                def turn(t):
                    for stage in (turn_x, sum_all, layer1, layer2, layer3):
                        stage(t)
                general_turns(pe, turn)

            two_paths(pe, fast, general)


_INS = ["x", "dst", "edge_attr_128", "L0_gnn_W1", "L0_gnn_b1", "L0_gnn_W2", "L0_gnn_b2", "L0_gnn_W3", "L0_gnn_b3",
        "L0_gnn_ln_gamma", "L0_gnn_ln_beta"]


def kernel(**inputs):
    import numpy as _np
    import concourse.bacc as _bacc
    from concourse import mybir as _mybir
    from concourse.bass_utils import run_bass_kernel_spmd as _run

    nc = _bacc.Bacc("TRN2", target_bir_lowering=False, num_devices=1)
    arrays, args = {}, []
    for name in _INS:
        a = _np.ascontiguousarray(inputs[name])
        arrays[f"in_{name}_dram"] = a
        args.append(nc.dram_tensor(f"in_{name}_dram", a.shape, _mybir.dt.from_np(a.dtype), kind="ExternalInput").ap())
    shape = _np.shape(inputs["x"])
    args.append(nc.dram_tensor("out_0_dram", shape, _mybir.dt.from_np(_np.dtype("float32")),
                               kind="ExternalOutput").ap())
    gnn_layer(nc, *args)
    r = _run(nc, [arrays], core_ids=[0])
    return r.results[0]["out_0_dram"]
```

```python
from contextlib import ExitStack

import concourse.bass as bass
from concourse import mybir

P = 128
ALU = mybir.AluOpType
ACT = mybir.ActivationFunctionType
AX_X = mybir.AxisListType.X
F32 = mybir.dt.float32
BF16 = mybir.dt.bfloat16
I32 = mybir.dt.int32
F32R = mybir.dt.float32r

ROWS = 4
GROUP = P * ROWS
WIN_NODES = 64
WINS = GROUP // WIN_NODES
BLOCK = 16
EPS = 1e-5

UNROLL = 4
ACT_ROWS = 2
X_BUFS = 4
EDGE_BUFS = 4
OUT_BUFS = 4
PAIR = 2
KEEP = 8
LOOP_FROM = 6
LOAD_X_AHEAD = 4
LOAD_E_AHEAD = 4

GEN_COLS = 10
GEN_EDGE_BUFS = 4


class Turn:

    def __init__(self, g, phase=None, whole=None, general=False):
        self.g, self.phase, self.whole, self.general = g, phase, whole, general

    def ring(self, n):
        return 0 if self.general else self.phase % n

    def round(self, n):
        if self.general:
            return self.g
        return self.whole * (UNROLL // n) + self.phase // n

    def depth(self, n):
        return 1 if self.general else n


def wait_count(eng, sem, value):
    if isinstance(value, int) and value <= 0:
        return
    eng.wait_ge(sem, value)


def gnn_layer(nc, x, dst, edge, w1_dram, b1, w2, b2, w3, b3, gamma, beta, out):
    N, D = x.shape
    E = edge.shape[0]
    assert D == P and N % ROWS == 0 and E % BLOCK == 0
    GROUPS = -(-N // GROUP)
    LAST = GROUPS - 1
    LAST_BASE = N - GROUP
    LAST_SKIP = (LAST * GROUP - LAST_BASE) // ROWS
    DST_PARTS = 125
    RUN = E // DST_PARTS
    RUN_BLOCKS = RUN // BLOCK
    assert E % DST_PARTS == 0 and RUN % BLOCK == 0 and GROUPS <= P
    assert N <= 1 << 16 and RUN_BLOCKS < 1 << 8
    LAST_BLOCK = (E - P) // BLOCK
    TABLE = LAST_BLOCK + 1
    BOUNDS = WINS + 1
    SPAN = P // BLOCK
    GEN_BATCHES = RUN // GEN_COLS
    assert RUN % GEN_COLS == 0 and GEN_BATCHES % GEN_EDGE_BUFS == 0
    LOOP_TURNS = (LAST - 6 - LOOP_FROM) // UNROLL * UNROLL
    LOOP_TO = LOOP_FROM + LOOP_TURNS

    x_rows = x.rearrange("(q r) f -> q (r f)", r=ROWS)
    out_rows = out.rearrange("(q r) f -> q (r f)", r=ROWS)
    dst_runs = dst.rearrange("(q j) -> q j", j=RUN)
    edge_runs = edge.rearrange("(q j) f -> q (j f)", j=RUN)
    dst_table = nc.dram_tensor("dst_table", [TABLE, P], I32, kind="Internal").ap()

    with ExitStack() as ctx:
        def sb(name, shape, dt=F32):
            return ctx.enter_context(nc.sbuf_tensor(name, shape, dt))

        def ps(name, shape=(P, GROUP), dt=F32):
            return ctx.enter_context(nc.psum_tensor(name, list(shape), dt))

        def sem(name):
            return ctx.enter_context(nc.semaphore(name))

        w1 = sb("w1", [P, 2, P])
        w1_hi = sb("w1_hi", [P, 2, P], F32R)
        w1_lo = sb("w1_lo", [P, 2, P], F32R)
        w2s = sb("w2s", [P, P])
        w3s = sb("w3s", [P, P])
        w3c = sb("w3c", [P, P])
        w3mean = sb("w3mean", [P, 1])
        b1c = sb("b1c", [P, 1])
        b2c = sb("b2c", [P, 1])
        b3r = sb("b3r", [1, P])
        b3mean = sb("b3mean", [1, 1])
        b3c = sb("b3c", [1, P])
        b3left = sb("b3left", [1, P])
        b3parts = sb("b3parts", [1, 3, P], BF16)
        b3rows = sb("b3rows", [3, P], BF16)
        ones_bf = sb("ones_bf", [3, P], BF16)
        gamma_all = sb("gamma_all", [P, P])
        beta_all = sb("beta_all", [P, P])
        eps_col = sb("eps_col", [P, 1])
        ones_col = sb("ones_col", [P, 1])
        run_blocks_col = sb("run_blocks_col", [P, 1], BF16)
        ones_bf_col = sb("ones_bf_col", [P, 1], BF16)
        ident = sb("ident", [P, P])
        local_node = sb("local_node", [P, ROWS, WIN_NODES // ROWS])

        dst_i = sb("dst_i", [DST_PARTS, RUN], I32)
        dst_f = sb("dst_f", [DST_PARTS, RUN])
        next_i = sb("next_i", [DST_PARTS, 1], I32)
        first_f = sb("first_f", [DST_PARTS, 1])
        next_f = sb("next_f", [DST_PARTS, 1])
        bound_row = sb("bound_row", [DST_PARTS, GROUPS, BOUNDS])
        block_hi = sb("block_hi", [DST_PARTS, RUN_BLOCKS], BF16)
        block_lo = sb("block_lo", [DST_PARTS, RUN_BLOCKS], BF16)
        past_first = sb("past_first", [DST_PARTS, GROUPS, BOUNDS], BF16)
        run_pick = sb("run_pick", [DST_PARTS, GROUPS, BOUNDS], BF16)
        past_block = sb("past_block", [RUN_BLOCKS, GROUPS, BOUNDS], BF16)
        start_f = sb("start_f", [1, GROUPS, WINS])
        start_i = sb("start_i", [1, GROUPS, WINS], I32)
        block_f = sb("block_f", [GROUPS, WINS])
        block_clamped = sb("block_clamped", [GROUPS, WINS])
        block_i = sb("block_i", [GROUPS, WINS], I32)
        base_col = sb("base_col", [GROUPS, 1])
        bound_step = sb("bound_step", [GROUPS, WINS])
        bound_col = sb("bound_col", [GROUPS, WINS])
        too_far = sb("too_far", [GROUPS, WINS])
        falls = sb("falls", [DST_PARTS, RUN])
        bad = sb("bad", [P, 2])
        bad_i = sb("bad_i", [1, 1], I32)
        bad_f = sb("bad_f", [1, 1])
        dst_win = sb("dst_win", [GROUPS, WINS, P], I32)
        dst_rel = sb("dst_rel", [GROUPS, WINS, P])
        dst_loc = sb("dst_loc", [P, GROUPS, WINS])

        x_in = sb("x_in", [P, X_BUFS, GROUP])
        x_keep = sb("x_keep", [P, KEEP, GROUP])
        edges = sb("edges", [P, EDGE_BUFS, WINS, P])
        stats = sb("stats", [P, PAIR, ROWS, 6])
        mean_var = sb("mean_var", [P, PAIR, ROWS, 2])
        std1 = sb("std1", [P, PAIR, ROWS])
        rstd1 = sb("rstd1", [P, PAIR, ROWS])
        x_hat = sb("x_hat", [P, PAIR, ROWS, P])
        one_hot = sb("one_hot", [P, PAIR, WINS, WIN_NODES])
        neg_mean = sb("neg_mean", [P, PAIR, ACT_ROWS])
        x_hi = sb("x_hi", [P, PAIR, GROUP], F32R)
        x_lo = sb("x_lo", [P, PAIR, GROUP], F32R)
        agg_hi = sb("agg_hi", [P, PAIR, GROUP], F32R)
        agg_lo = sb("agg_lo", [P, PAIR, GROUP], F32R)
        h1 = sb("h1", [P, PAIR, GROUP])
        h2 = sb("h2", [P, PAIR, GROUP])
        squares = sb("squares", [P, ROWS, P])
        sum_sq = sb("sum_sq", [P, PAIR, ROWS])
        std2 = sb("std2", [P, PAIR, ROWS])
        rstd2 = sb("rstd2", [P, PAIR, ROWS])
        result = sb("result", [P, OUT_BUFS, ROWS, P])

        gen_edges = sb("gen_edges", [DST_PARTS, GEN_EDGE_BUFS, GEN_COLS, P])
        gen_hot = sb("gen_hot", [DST_PARTS, PAIR, GEN_COLS, GROUP])
        gen_rel = sb("gen_rel", [DST_PARTS, RUN])
        group_node = sb("group_node", [DST_PARTS, WINS, ROWS, WIN_NODES // ROWS])
        zeros = sb("zeros", [P, GROUP])

        x_ps = [ps(f"x_ps{i}") for i in range(PAIR)]
        agg_ps = [ps(f"agg_ps{i}") for i in range(PAIR)]
        h1_ps = ps("h1_ps")
        h2_ps = ps("h2_ps")
        y_ps = [ps(f"y_ps{i}") for i in range(PAIR)]

        s_dst = sem("dst_loaded")
        s_next = sem("next_loaded")
        s_table = sem("table_written")
        s_weights = sem("weights_loaded")
        s_consts = sem("consts_made")
        s_iota = sem("bounds_made")
        s_ident0 = sem("ident_cleared")
        s_prep = sem("weights_prepared")
        s_b3 = sem("b3_rows_placed")
        s_split = sem("w1_split")
        s_ix = sem("index_steps")
        s_pick = sem("blocks_picked")
        s_rank = sem("ranks_counted")
        s_win = [sem(f"dst_windows_loaded{i}") for i in range(2)]
        s_rel = sem("dst_rel_ready")
        s_turned = sem("dst_turned")
        s_badsum = sem("bad_summed")

        s_x = [sem(f"x_loaded{i}") for i in range(X_BUFS // 2)]
        s_e = [sem(f"edges_loaded{i}") for i in range(EDGE_BUFS)]
        s_stored = [sem(f"stored{i}") for i in range(OUT_BUFS)]
        s_stats = sem("stats_ready")
        s_var = sem("var_ready")
        s_std1 = sem("std1_ready")
        s_rstd1 = sem("rstd1_ready")
        s_hat = sem("x_hat_ready")
        s_keep = sem("x_keep_ready")
        s_hot = sem("one_hot_ready")
        s_xps = sem("x_ps_ready")
        s_aggps = sem("agg_ps_ready")
        s_hat_act = sem("x_hat_rows_ready")
        s_nmean = sem("neg_mean_ready")
        s_xhi = sem("x_hi_ready")
        s_xlo = sem("x_lo_ready")
        s_agghi = sem("agg_hi_ready")
        s_agglo = sem("agg_lo_ready")
        s_h1ps = sem("h1_ps_ready")
        s_h1 = sem("h1_ready")
        s_h2ps = sem("h2_ps_ready")
        s_h2 = sem("h2_ready")
        s_yps = sem("y_ps_ready")
        s_sq = sem("sum_sq_ready")
        s_std2 = sem("std2_ready")
        s_rstd2 = sem("rstd2_ready")
        s_scaled = sem("scaled_ready")
        s_out = sem("out_ready")

        s_ge = [sem(f"gen_edges_loaded{i}") for i in range(GEN_EDGE_BUFS)]
        s_ghot = sem("gen_hot_ready")
        s_gmm = sem("gen_batches_summed")
        s_grel = sem("gen_rel_steps")

        WEIGHT_LOADS = 9
        HALF = GROUPS // 2
        assert GROUPS % 2 == 0 and HALF * BOUNDS <= 512

        def all_turns(eng, turn):
            for i in range(-4, LOOP_FROM):
                turn(lambda ahead, i=i: Turn(i + ahead, i + ahead, 0))
            with eng.Fori(0, LOOP_TURNS // UNROLL) as j:
                first = eng.snap(j * UNROLL)
                for u in range(UNROLL):
                    phase = LOOP_FROM + u
                    turn(lambda ahead, u=u, phase=phase: Turn(first + (phase + ahead), phase + ahead, j))
            for i in range(LOOP_TO, GROUPS + 4):
                turn(lambda ahead, i=i: Turn(i + ahead, i + ahead, 0))

        def there(t):
            return not isinstance(t.g, int) or 0 <= t.g < GROUPS

        def is_first(t):
            return isinstance(t.g, int) and t.g == 0

        def is_preloaded(t):
            return isinstance(t.g, int) and t.g < (1 if t.general else X_BUFS)

        def is_last(t):
            return isinstance(t.g, int) and t.g == LAST

        def x_loads(t):
            own_last = not t.general and isinstance(t.g, int) and t.g >= LAST - 1
            return (t.round(X_BUFS) + 1) * 16 + (16 if own_last else 0)

        def by_window(ap):
            return ap.rearrange("p (r w c) -> p w r c", r=ROWS, w=WINS)

        def sums(t):
            return agg_ps[t.ring(PAIR)][:, :].rearrange("p (w r c) -> p w r c", r=ROWS, w=WINS)

        def two_paths(eng, fast, general):
            eng.wait_ge(s_ix, IX_DONE)
            flag = eng.value_load(bad_i[0:1, 0:1], min_val=0, max_val=2 * P)
            with eng.If(flag < 1):
                fast()
            with eng.Else():
                general()

        def general_turns(eng, turn):
            turn(Turn(0, general=True))
            with eng.Fori(1, LAST) as g:
                turn(Turn(g, general=True))
            turn(Turn(LAST, general=True))

        IX_DONE = 17
        PREPARED = 10
        BLOCKS_FOUND = 12

        block = ctx.enter_context(nc.Block())

        @block.sync
        def _(sp):
            sp.dma_start(dst_i[:, :], dst_runs).then_inc(s_dst, 16)
            with nc.allow_non_contiguous_dma("one first dst of each run"):
                sp.dma_start(next_i[0:DST_PARTS - 1, :], dst_runs[1:DST_PARTS, 0:1]).then_inc(s_next, 16)
            rows = TABLE // 16 * 16
            for r0, r1 in ((0, rows), (rows, TABLE)):
                src = bass.AP(dst.tensor, BLOCK * r0, [[BLOCK, r1 - r0], [1, P]])
                sp.dma_start(dst_table[r0:r1, :], src).then_inc(s_table, 16)
            for tile, src in ((w1[:, 0, :], w1_dram[0:P, :]), (w1[:, 1, :], w1_dram[P:2 * P, :]),
                              (w2s[:, :], w2), (w3s[:, :], w3)):
                sp.dma_start(tile, src).then_inc(s_weights, 16)
            with nc.allow_non_contiguous_dma("a bias is a column"):
                for tile, src in ((b1c, b1), (b2c, b2)):
                    sp.dma_start(tile[:, :], src.rearrange("(p o) -> p o", o=1)).then_inc(s_weights, 16)
            sp.dma_start(b3r[:, :], b3.rearrange("(o f) -> o f", o=1)).then_inc(s_weights, 16)
            for tile, src in ((gamma_all, gamma), (beta_all, beta)):
                sp.dma_start(tile[:, :], bass.AP(src.tensor, 0, [[0, P], [1, P]])).then_inc(s_weights, 16)
            for g in range(0, X_BUFS, 2):
                sp.dma_start(x_in[:, g:g + 2, :],
                             x_rows[g * P:(g + 2) * P, :].rearrange("(k p) f -> p k f", k=2)) \
                    .then_inc(s_x[g // 2], 16)

            def load_x(t):
                if not there(t) or is_preloaded(t):
                    return
                wait_count(sp, s_hat, t.g - t.depth(X_BUFS) + 1)
                wait_count(sp, s_hat_act, t.g - t.depth(X_BUFS) + 1)
                wait_count(sp, s_keep, t.g - t.depth(X_BUFS) + 1)
                row = LAST_BASE // ROWS if is_last(t) else t.g * P
                sp.dma_start(x_in[:, t.ring(X_BUFS), :], x_rows[bass.ds(row, P), :]) \
                    .then_inc(s_x[t.ring(X_BUFS) // 2], 16)

            def load_x_pair(at, ahead):
                t, t2 = at(ahead), at(ahead + 1)
                if t.phase % 2 or not there(t) or is_preloaded(t):
                    return
                if is_last(t2):
                    load_x(t)
                    load_x(t2)
                    return
                wait_count(sp, s_hat, t2.g - X_BUFS + 1)
                wait_count(sp, s_hat_act, t2.g - X_BUFS + 1)
                wait_count(sp, s_keep, t2.g - X_BUFS + 1)
                slot = t.ring(X_BUFS)
                sp.dma_start(x_in[:, slot:slot + 2, :],
                             x_rows[bass.ds(t.g * P, 2 * P), :].rearrange("(k p) f -> p k f", k=2)) \
                    .then_inc(s_x[slot // 2], 16)

            def load_edges(t):
                if not there(t):
                    return
                wait_count(sp, s_aggps, t.g - EDGE_BUFS + 1)
                _, starts = nc.values_load_multi_w_load_instructions(
                    start_i[0:1, bass.ds(t.g, 1), :].rearrange("o g w -> o (g w)"), engines=[sp.engine],
                    min_val=0, max_val=E - P, skip_runtime_bounds_check_because="the index stage keeps starts within 0 and E - P")
                for w in range(WINS):
                    sp.dma_start(edges[:, t.ring(EDGE_BUFS), w, :], edge[bass.ds(starts[w], P), :]) \
                        .then_inc(s_e[t.ring(EDGE_BUFS)], 16)

            def fast():
                def turn(at):
                    load_x_pair(at, LOAD_X_AHEAD)
                    load_edges(at(LOAD_E_AHEAD))
                all_turns(sp, turn)

            def general():
                def turn(t):
                    load_x(t)
                    with sp.Fori(0, GEN_BATCHES // GEN_EDGE_BUFS) as k:
                        for b in range(GEN_EDGE_BUFS):
                            sp.wait_ge(s_gmm, t.g * GEN_BATCHES + k * GEN_EDGE_BUFS + (b + 1))
                            sp.dma_start(gen_edges[:, b, :, :].rearrange("p c f -> p (c f)"),
                                         edge_runs[:, bass.ds((k * GEN_EDGE_BUFS + b) * GEN_COLS * P, GEN_COLS * P)]) \
                                .then_inc(s_ge[b], 16)
                general_turns(sp, turn)

            two_paths(sp, fast, general)

        @block.gpsimd
        def _(pool):
            pool.iota(bound_row[:, 0:LAST, :], [[GROUP, LAST], [WIN_NODES, BOUNDS]], base=0,
                      channel_multiplier=0, allow_small_or_imprecise_dtypes=True)
            pool.iota(bound_row[:, LAST:GROUPS, :], [[0, 1], [WIN_NODES, BOUNDS]], base=LAST_BASE,
                      channel_multiplier=0, allow_small_or_imprecise_dtypes=True).then_inc(s_iota, 1)
            pool.memset(ident[:, :], 0.0).then_inc(s_ident0, 1)
            pool.wait_ge(s_ident0, 1)
            pool.affine_select(out=ident[:, :], in_=ident[:, :], compare_op=ALU.not_equal, fill=1.0,
                               base=0, pattern=[[-1, P]], channel_multiplier=1)
            pool.iota(base_col[:, :], [[0, 1]], base=0, channel_multiplier=GROUP,
                      allow_small_or_imprecise_dtypes=True)
            pool.iota(bound_step[:, :], [[WIN_NODES, WINS]], base=0, channel_multiplier=0,
                      allow_small_or_imprecise_dtypes=True)
            pool.iota(local_node[:, :, :], [[1, ROWS], [ROWS, WIN_NODES // ROWS]], base=0,
                      channel_multiplier=0, allow_small_or_imprecise_dtypes=True)
            pool.iota(group_node[:, :, :, :], [[WIN_NODES, WINS], [1, ROWS], [ROWS, WIN_NODES // ROWS]], base=0,
                      channel_multiplier=0, allow_small_or_imprecise_dtypes=True).then_inc(s_consts, 1)
            pool.wait_ge(s_table, 32)
            pool.wait_ge(s_ix, BLOCKS_FOUND)
            for w in range(WINS):
                pool.indirect_dma_start(
                    out=dst_win[:, w, :], out_offset=None, in_=dst_table[:, :],
                    in_offset=bass.IndirectOffsetOnAxis(ap=block_i[:, w:w + 1], axis=0)) \
                    .then_inc(s_win[w // 4], 16)
            for half in range(2):
                pool.wait_ge(s_win[half], 16 * 4)
            pool.wait_ge(s_weights, 16 * WEIGHT_LOADS)

            def keep_x(t):
                if not there(t):
                    return
                pool.wait_ge(s_x[t.ring(X_BUFS) // 2], x_loads(t))
                wait_count(pool, s_out, t.g - t.depth(KEEP) + 1)
                pool.tensor_tensor(kept(t), x_in[:, t.ring(X_BUFS), :].rearrange("p (r f) -> p r f", r=ROWS),
                                   beta_all[:, :].unsqueeze(1).to_broadcast([P, ROWS, P]), ALU.add) \
                    .then_inc(s_keep, 1)

            def kept(t):
                slot = t.g % KEEP if isinstance(t.g, int) else t.g & (KEEP - 1)
                if t.general:
                    slot = 0
                return x_keep[:, bass.ds(slot, 1), :].rearrange("p o (r f) -> p (o r) f", r=ROWS)

            def add_x(t):
                if not there(t):
                    return
                pool.wait_ge(s_scaled, t.g + 1)
                pool.wait_ge(s_keep, t.g + 1)
                r = result[:, t.ring(OUT_BUFS), :, :]
                pool.tensor_tensor(r, r, kept(t), ALU.add).then_inc(s_out, 1)

            def store(t):
                if not there(t):
                    return
                pool.wait_ge(s_out, t.g + 1)
                skip = LAST_SKIP if is_last(t) else 0
                row = LAST_BASE // ROWS + skip if is_last(t) else t.g * P
                pool.dma_start(out_rows[bass.ds(row, P - skip), :],
                               result[skip:P, t.ring(OUT_BUFS), :, :].rearrange("p r f -> p (r f)")) \
                    .then_inc(s_stored[t.ring(OUT_BUFS)], 16)

            def fast():
                def turn(at):
                    keep_x(at(3))
                    add_x(at(-2))
                    store(at(-2))
                all_turns(pool, turn)
                for i in range(OUT_BUFS):
                    pool.wait_ge(s_stored[i], 16 * len(range(i, GROUPS, OUT_BUFS)))

            def general():
                def turn(t):
                    keep_x(t)
                    add_x(t)
                    store(t)
                general_turns(pool, turn)
                pool.wait_ge(s_stored[0], 16 * GROUPS)

            two_paths(pool, fast, general)

        @block.scalar
        def _(act):
            act.wait_ge(s_prep, 8)
            for k in range(3):
                act.dma_start(b3rows[k:k + 1, :], b3parts[0:1, k, :]).then_inc(s_b3, 16)
            act.wait_ge(s_weights, 16 * WEIGHT_LOADS)

            def std_x(t):
                if not there(t):
                    return
                act.wait_ge(s_var, t.g + 1)
                wait_count(act, s_rstd1, t.g - t.depth(PAIR) + 1)
                act.activation(std1[:, t.ring(PAIR), :], mean_var[:, t.ring(PAIR), :, 1], ACT.Sqrt,
                               bias=eps_col[:, :]).then_inc(s_std1, 1)

            def normalise_rows(t):
                if not there(t):
                    return
                act.wait_ge(s_nmean, t.g + 1)
                wait_count(act, s_xps, t.g - t.depth(PAIR) + 1)
                for r in range(ACT_ROWS):
                    last = act.activation(x_hat[:, t.ring(PAIR), r, :],
                                          x_in[:, t.ring(X_BUFS), r * P:(r + 1) * P], ACT.Identity,
                                          bias=neg_mean[:, t.ring(PAIR), r:r + 1],
                                          scale=rstd1[:, t.ring(PAIR), r:r + 1])
                last.then_inc(s_hat_act, 1)

            def relu_x(t):
                if not there(t):
                    return
                act.wait_ge(s_xps, t.g + 1)
                wait_count(act, s_h1ps, t.g - t.depth(PAIR) + 1)
                act.activation(x_hi[:, t.ring(PAIR), :], x_ps[t.ring(PAIR)][:, :], ACT.Relu).then_inc(s_xhi, 1)

            def copy_agg(t):
                if not there(t):
                    return
                act.wait_ge(s_aggps, t.g + 1)
                wait_count(act, s_h1ps, t.g - t.depth(PAIR) + 1)
                act.activation(by_window(agg_hi[:, t.ring(PAIR), :]), sums(t), ACT.Copy).then_inc(s_agghi, 1)

            def relu_h1(t):
                if not there(t):
                    return
                act.wait_ge(s_h1ps, t.g + 1)
                wait_count(act, s_h2ps, t.g - t.depth(PAIR) + 1)
                act.activation(h1[:, t.ring(PAIR), :], h1_ps[:, :], ACT.Relu, bias=b1c[:, :]).then_inc(s_h1, 1)

            def relu_h2(t):
                if not there(t):
                    return
                act.wait_ge(s_h2ps, t.g + 1)
                wait_count(act, s_yps, t.g - t.depth(PAIR) + 1)
                act.activation(h2[:, t.ring(PAIR), :], h2_ps[:, :], ACT.Relu, bias=b2c[:, :]).then_inc(s_h2, 1)

            def sum_squares(t):
                if not there(t):
                    return
                act.wait_ge(s_yps, t.g + 1)
                for r in range(ROWS):
                    last = act.activation(squares[:, r, :], y_ps[t.ring(PAIR)][:, r * P:(r + 1) * P], ACT.Square,
                                          accum_out=sum_sq[:, t.ring(PAIR), r:r + 1])
                last.then_inc(s_sq, 1)

            def std_y(t):
                if not there(t):
                    return
                act.wait_ge(s_sq, t.g + 1)
                wait_count(act, s_rstd2, t.g - t.depth(PAIR) + 1)
                act.activation(std2[:, t.ring(PAIR), :], sum_sq[:, t.ring(PAIR), :], ACT.Sqrt,
                               bias=eps_col[:, :], scale=1.0 / D).then_inc(s_std2, 1)

            def fast():
                def turn(at):
                    sum_squares(at(-2))
                    std_y(at(-2))
                    relu_h1(at(0))
                    relu_x(at(1))
                    copy_agg(at(1))
                    std_x(at(3))
                    normalise_rows(at(2))
                    relu_h2(at(0))
                all_turns(act, turn)

            def general():
                def turn(t):
                    for stage in (std_x, normalise_rows, relu_x, copy_agg, relu_h1, relu_h2, sum_squares, std_y):
                        stage(t)
                general_turns(act, turn)

            two_paths(act, fast, general)

        @block.vector
        def _(dve):
            steps = [0]

            def step(ins):
                steps[0] += 1
                ins.then_inc(s_ix, 1)
                dve.wait_ge(s_ix, steps[0])

            def half_of(ap, half):
                return ap[:, half * HALF:(half + 1) * HALF, :]

            dve.memset(ones_col[:, :], 1.0)
            dve.memset(ones_bf_col[:, :], 1.0)
            dve.memset(run_blocks_col[:, :], float(RUN_BLOCKS))
            dve.memset(bad[:, :], 0.0)
            dve.memset(eps_col[:, :], EPS)
            dve.memset(ones_bf[:, :], 1.0)
            dve.memset(zeros[:, :], 0.0)
            step(dve.memset(next_f[:, :], float(N)))
            dve.wait_ge(s_dst, 16)
            dve.wait_ge(s_next, 16)
            dve.tensor_copy(next_f[0:DST_PARTS - 1, :], next_i[0:DST_PARTS - 1, :])
            dve.tensor_copy(block_hi[:, :], dst_i[:, 0:RUN:BLOCK])
            dve.tensor_copy(first_f[:, :], dst_i[:, 0:1])
            step(dve.tensor_copy(dst_f[:, :], dst_i[:, :]))
            dve.tensor_tensor(block_lo[:, :], dst_f[:, 0:RUN:BLOCK], block_hi[:, :], ALU.subtract)
            step(dve.memset(first_f[0:1, :], -1.0))
            dve.wait_ge(s_iota, 1)
            for half in range(2):
                step(dve.tensor_scalar(half_of(past_first, half), half_of(bound_row, half), first_f[:, 0:1], None,
                                       ALU.is_gt))
                step(dve.scalar_tensor_tensor(out=half_of(run_pick, half), in0=half_of(bound_row, half),
                                              scalar=next_f[:, 0:1], in1=half_of(past_first, half),
                                              op0=ALU.is_le, op1=ALU.mult))
            assert steps[0] == 7
            for half in range(2):
                dve.wait_ge(s_pick, half + 1)
                last = dve.tensor_tensor(
                    half_of(past_block, half),
                    x_ps[half][0:RUN_BLOCKS, 0:HALF * BOUNDS].rearrange("p (g b) -> p g b", b=BOUNDS),
                    half_of(bound_row, half)[0:RUN_BLOCKS], ALU.is_lt)
            step(last)
            assert steps[0] == 8
            dve.tensor_tensor(falls[:, RUN - 1:RUN], dst_f[:, RUN - 1:RUN], next_f[:, :], ALU.is_gt)
            step(dve.tensor_tensor(falls[:, 0:RUN - 1], dst_f[:, 0:RUN - 1], dst_f[:, 1:RUN], ALU.is_gt))
            step(dve.tensor_reduce(bad[0:DST_PARTS, 1:2], falls[:, :], AX_X, ALU.max))
            dve.wait_ge(s_rank, 1)
            step(dve.tensor_scalar(block_f[:, :], agg_ps[0][0:GROUPS, 0:BOUNDS][:, 0:WINS], -float(RUN_BLOCKS + 1),
                                   0.0, ALU.add, ALU.max))
            step(dve.tensor_scalar(block_i[:, :], block_f[:, :], float(LAST_BLOCK), None, ALU.min))
            assert steps[0] == BLOCKS_FOUND
            step(dve.tensor_scalar(block_clamped[:, :], block_f[:, :], float(LAST_BLOCK), None, ALU.min))
            step(dve.scalar_tensor_tensor(out=too_far[:, :], in0=agg_ps[0][0:GROUPS, 1:BOUNDS],
                                          scalar=-(SPAN + RUN_BLOCKS + 0.5), in1=block_clamped[:, :],
                                          op0=ALU.add, op1=ALU.is_gt))
            dve.tensor_reduce(bad[0:GROUPS, 0:1], too_far[:, :], AX_X, ALU.max)
            dve.wait_ge(s_rank, 2)
            for half in range(2):
                rows = (h1_ps, h2_ps)[half][0:1, 0:HALF * BOUNDS].rearrange("p (g b) -> p g b", b=BOUNDS)
                last = dve.tensor_scalar(half_of(start_f, half), rows[:, :, 0:WINS],
                                         -float(RUN_BLOCKS + 1), 0.0, ALU.add, ALU.max)
            step(last)
            step(dve.tensor_scalar(start_i[:, :, :], start_f[:, :, :], float(LAST_BLOCK), float(BLOCK),
                                   ALU.min, ALU.mult))
            assert steps[0] == IX_DONE - 1
            dve.wait_ge(s_badsum, 1)
            dve.tensor_reduce(bad_f[:, :], agg_ps[1][0:1, 0:2], AX_X, ALU.add).then_inc(s_prep, 1)
            dve.wait_ge(s_prep, 1)
            step(dve.tensor_copy(bad_i[:, :], bad_f[:, :]))
            assert steps[0] == IX_DONE

            dve.wait_ge(s_weights, 16 * WEIGHT_LOADS)
            dve.tensor_reduce(b3mean[:, :], b3r[:, :], AX_X, ALU.add)
            dve.tensor_reduce(w3mean[:, :], w3s[:, :], AX_X, ALU.add).then_inc(s_prep, 1)
            dve.wait_ge(s_prep, 2)
            dve.tensor_scalar(b3mean[:, :], b3mean[:, :], 1.0 / D, None, ALU.mult)
            dve.tensor_scalar(w3mean[:, :], w3mean[:, :], 1.0 / D, None, ALU.mult).then_inc(s_prep, 1)
            dve.wait_ge(s_prep, 3)
            dve.tensor_scalar(w3c[:, :], w3s[:, :], w3mean[:, 0:1], None, ALU.subtract)
            dve.tensor_scalar(b3c[:, :], b3r[:, :], b3mean[:, 0:1], None, ALU.subtract).then_inc(s_prep, 1)
            dve.wait_ge(s_prep, 4)
            dve.tensor_copy(b3parts[:, 0, :], b3c[:, :]).then_inc(s_prep, 1)
            dve.wait_ge(s_prep, 5)
            dve.tensor_tensor(b3left[:, :], b3c[:, :], b3parts[:, 0, :], ALU.subtract).then_inc(s_prep, 1)
            dve.wait_ge(s_prep, 6)
            dve.tensor_copy(b3parts[:, 1, :], b3left[:, :]).then_inc(s_prep, 1)
            dve.wait_ge(s_prep, 7)
            dve.tensor_tensor(b3parts[:, 2, :], b3left[:, :], b3parts[:, 1, :], ALU.subtract).then_inc(s_prep, 1)

            dve.tensor_copy(w1_hi[:, :, :], w1[:, :, :]).then_inc(s_split, 1)
            dve.wait_ge(s_split, 1)
            dve.tensor_tensor(w1_lo[:, :, :], w1[:, :, :], w1_hi[:, :, :].bitcast(F32), ALU.subtract) \
                .then_inc(s_split, 1)

            dve.wait_ge(s_consts, 1)
            dve.tensor_scalar(base_col[:, :], base_col[:, :], float(LAST_BASE), None, ALU.min).then_inc(s_prep, 1)
            dve.wait_ge(s_prep, 9)
            dve.tensor_scalar(bound_col[:, :], bound_step[:, :], base_col[:, 0:1], None, ALU.add).then_inc(s_prep, 1)
            dve.wait_ge(s_prep, 10)

            def locate_edge_rows():
                for half in range(2):
                    wins = slice(half * 4, half * 4 + 4)
                    dve.wait_ge(s_win[half], 16 * 4)
                    dve.tensor_tensor(dst_rel[:, wins, :], dst_win[:, wins, :],
                                      bound_col[:, wins].unsqueeze(2).to_broadcast([GROUPS, 4, P]),
                                      ALU.subtract).then_inc(s_rel, 1)
                for half in range(2):
                    dve.wait_ge(s_turned, half + 1)
                    last = dve.tensor_copy(
                        dst_loc[:, :, half * 4:half * 4 + 4].rearrange("p g w -> p w g"),
                        y_ps[half][:, 0:4 * GROUPS].rearrange("p (w g) -> p w g", w=4))
                last.then_inc(s_rel, 1)
                dve.wait_ge(s_rel, 3)

            def x_rows_of(t):
                return x_in[:, t.ring(X_BUFS), :].rearrange("p (r f) -> p r f", r=ROWS)

            def x_stats(t):
                if not there(t):
                    return
                dve.wait_ge(s_x[t.ring(X_BUFS) // 2], x_loads(t))
                for r in range(ROWS):
                    last = dve.bn_stats(stats[:, t.ring(PAIR), r, :], x_rows_of(t)[:, r, :])
                last.then_inc(s_stats, 1)
                dve.wait_ge(s_stats, t.g + 1)

            def x_mean_var(t):
                if not there(t):
                    return
                for r in range(ROWS):
                    last = dve.bn_aggr(mean_var[:, t.ring(PAIR), r, :], stats[:, t.ring(PAIR), r, :])
                last.then_inc(s_var, 1)

            def reciprocal_x(t):
                if not there(t):
                    return
                dve.wait_ge(s_std1, t.g + 1)
                wait_count(dve, s_hat_act, t.g - t.depth(PAIR) + 1)
                dve.reciprocal(rstd1[:, t.ring(PAIR), :], std1[:, t.ring(PAIR), :]).then_inc(s_rstd1, 1)
                dve.wait_ge(s_rstd1, t.g + 1)
                dve.scalar_tensor_tensor(out=neg_mean[:, t.ring(PAIR), :], in0=mean_var[:, t.ring(PAIR), 0:ACT_ROWS, 0],
                                         scalar=-1.0, in1=rstd1[:, t.ring(PAIR), 0:ACT_ROWS],
                                         op0=ALU.mult, op1=ALU.mult).then_inc(s_nmean, 1)

            def normalise(t):
                if not there(t):
                    return
                wait_count(dve, s_xps, t.g - t.depth(PAIR) + 1)
                for r in range(ACT_ROWS, ROWS):
                    last = dve.tensor_scalar(x_hat[:, t.ring(PAIR), r, :], x_rows_of(t)[:, r, :],
                                             mean_var[:, t.ring(PAIR), r, 0:1], rstd1[:, t.ring(PAIR), r:r + 1],
                                             ALU.subtract, ALU.mult)
                last.then_inc(s_hat, 1)

            def low_x(t):
                if not there(t):
                    return
                dve.wait_ge(s_xhi, t.g + 1)
                dve.scalar_tensor_tensor(out=x_lo[:, t.ring(PAIR), :], in0=x_ps[t.ring(PAIR)][:, :], scalar=0.0,
                                         in1=x_hi[:, t.ring(PAIR), :].bitcast(F32), op0=ALU.max,
                                         op1=ALU.subtract).then_inc(s_xlo, 1)

            def low_agg(t):
                if not there(t):
                    return
                dve.wait_ge(s_agghi, t.g + 1)
                dve.tensor_tensor(by_window(agg_lo[:, t.ring(PAIR), :]), sums(t),
                                  by_window(agg_hi[:, t.ring(PAIR), :].bitcast(F32)),
                                  ALU.subtract).then_inc(s_agglo, 1)

            def make_one_hot(t):
                if not there(t):
                    return
                wait_count(dve, s_aggps, t.g - PAIR + 1)
                dve.tensor_tensor(
                    one_hot[:, t.ring(PAIR), :, :],
                    local_node[:, :, :].rearrange("p r c -> p (r c)").unsqueeze(1).to_broadcast([P, WINS, WIN_NODES]),
                    dst_loc[:, bass.ds(t.g, 1), :].rearrange("p o w -> p (o w)").unsqueeze(2)
                    .to_broadcast([P, WINS, WIN_NODES]), ALU.is_equal).then_inc(s_hot, 1)

            def scale_y(t):
                if not there(t):
                    return
                dve.wait_ge(s_std2, t.g + 1)
                dve.reciprocal(rstd2[:, t.ring(PAIR), :], std2[:, t.ring(PAIR), :]).then_inc(s_rstd2, 1)
                dve.wait_ge(s_rstd2, t.g + 1)
                wait_count(dve, s_stored[t.ring(OUT_BUFS)], t.round(OUT_BUFS) * 16)
                for r in range(ROWS):
                    last = dve.scalar_tensor_tensor(
                        out=result[:, t.ring(OUT_BUFS), r, :], in0=y_ps[t.ring(PAIR)][:, r * P:(r + 1) * P],
                        scalar=rstd2[:, t.ring(PAIR), r:r + 1], in1=gamma_all[:, :], op0=ALU.mult, op1=ALU.mult)
                last.then_inc(s_scaled, 1)

            def fast():
                def turn(at):
                    x_stats(at(3))
                    scale_y(at(-2))
                    x_mean_var(at(3))
                    reciprocal_x(at(2))
                    low_x(at(1))
                    low_agg(at(1))
                    normalise(at(2))
                    if is_first(at(2)):
                        locate_edge_rows()
                    make_one_hot(at(2))
                all_turns(dve, turn)

            def general():
                dve.tensor_copy(gen_rel[:, :], dst_f[:, :]).then_inc(s_grel, 1)

                def turn(t):
                    x_stats(t)
                    dve.memset(bad_f[:, :], 0.0)
                    x_mean_var(t)
                    reciprocal_x(t)
                    normalise(t)
                    low_x(t)
                    dve.wait_ge(s_prep, PREPARED)
                    dve.wait_ge(s_grel, t.g + 1)
                    if is_last(t):
                        dve.tensor_scalar(gen_rel[:, :], gen_rel[:, :], float(LAST * GROUP - LAST_BASE), None,
                                          ALU.add).then_inc(s_grel, 1)
                        dve.wait_ge(s_grel, LAST + 2)
                    with dve.Fori(0, GEN_BATCHES // PAIR) as k:
                        for b in range(PAIR):
                            dve.wait_ge(s_gmm, t.g * GEN_BATCHES + k * PAIR + (b + GEN_EDGE_BUFS - PAIR + 1))
                            for c in range(GEN_COLS):
                                last = dve.tensor_scalar(
                                    gen_hot[:, b, c, :], group_node[:, :, :, :].rearrange("p w r c -> p (w r c)"),
                                    gen_rel[:, bass.ds((k * PAIR + b) * GEN_COLS + c, 1)], None, ALU.is_equal)
                            last.then_inc(s_ghot, 1)
                    if not is_last(t):
                        dve.wait_ge(s_ghot, (t.g + 1) * GEN_BATCHES)
                        dve.tensor_scalar(gen_rel[:, :], gen_rel[:, :], -float(GROUP), None,
                                          ALU.add).then_inc(s_grel, 1)
                    low_agg(t)
                    scale_y(t)
                general_turns(dve, turn)

            two_paths(dve, fast, general)

        @block.tensor
        def _(pe):
            for half in range(2):
                pick = x_ps[half][0:RUN_BLOCKS, 0:HALF * BOUNDS]
                runs = run_pick[:, half * HALF:(half + 1) * HALF, :].rearrange("p g b -> p (g b)")
                pe.wait_ge(s_ix, (5, 7)[half])
                pe.matmul(pick, block_hi[:, :], runs, start=True, stop=False)
                pe.matmul(pick, block_lo[:, :], runs, start=False, stop=True).then_inc(s_pick, 1)
            pe.wait_ge(s_ix, 8)
            for b in range(BOUNDS):
                pe.matmul(agg_ps[0][0:GROUPS, b:b + 1], past_first[:, :, b], run_blocks_col[0:DST_PARTS, :],
                          start=True, stop=False)
                last = pe.matmul(agg_ps[0][0:GROUPS, b:b + 1], past_block[:, :, b], ones_bf_col[0:RUN_BLOCKS, :],
                                 start=False, stop=True)
            last.then_inc(s_rank, 1)
            for half in range(2):
                part = slice(half * HALF, (half + 1) * HALF)
                row = (h1_ps, h2_ps)[half][0:1, 0:HALF * BOUNDS]
                pe.matmul(row, run_blocks_col[0:DST_PARTS, :], past_first[:, part, :].rearrange("p g b -> p (g b)"),
                          start=True, stop=False)
                last = pe.matmul(row, ones_bf_col[0:RUN_BLOCKS, :], past_block[:, part, :].rearrange("p g b -> p (g b)"),
                                 start=False, stop=True)
            last.then_inc(s_rank, 1)
            pe.wait_ge(s_ix, IX_DONE - 1)
            pe.matmul(agg_ps[1][0:1, 0:2], ones_col[:, :], bad[:, :], start=True, stop=True).then_inc(s_badsum, 1)
            pe.wait_ge(s_consts, 1)
            pe.wait_ge(s_prep, PREPARED)
            pe.wait_ge(s_split, 2)
            pe.wait_ge(s_b3, 48)
            pe.wait_ge(s_weights, 16 * WEIGHT_LOADS)

            def turn_dst():
                for half in range(2):
                    pe.wait_ge(s_rel, half + 1)
                    for w in range(4):
                        last = pe.transpose(y_ps[half][:, w * GROUPS:(w + 1) * GROUPS], dst_rel[:, half * 4 + w, :],
                                            ident[0:GROUPS, 0:GROUPS])
                    last.then_inc(s_turned, 1)

            def turn_x(t):
                if not there(t):
                    return
                pe.wait_ge(s_hat, t.g + 1)
                pe.wait_ge(s_hat_act, t.g + 1)
                wait_count(pe, s_xlo, t.g - t.depth(PAIR) + 1)
                for r in range(ROWS):
                    last = pe.transpose(x_ps[t.ring(PAIR)][:, r * P:(r + 1) * P], x_hat[:, t.ring(PAIR), r, :],
                                        ident[:, :])
                last.then_inc(s_xps, 1)

            def sum_windows(t):
                if not there(t):
                    return
                pe.wait_ge(s_hot, t.g + 1)
                pe.wait_ge(s_e[t.ring(EDGE_BUFS)], (t.round(EDGE_BUFS) + 1) * (16 * WINS))
                wait_count(pe, s_agglo, t.g - PAIR + 1)
                for w in range(WINS):
                    last = pe.matmul(agg_ps[t.ring(PAIR)][:, w * WIN_NODES:(w + 1) * WIN_NODES],
                                     edges[:, t.ring(EDGE_BUFS), w, :], one_hot[:, t.ring(PAIR), w, :],
                                     start=True, stop=True)
                last.then_inc(s_aggps, 1)

            def layer1(t):
                if not there(t):
                    return
                pe.wait_ge(s_xlo, t.g + 1)
                pe.wait_ge(s_agglo, t.g + 1)
                wait_count(pe, s_h1, t.g)
                for k, (hi, lo) in enumerate(((x_hi, x_lo), (agg_hi, agg_lo))):
                    pe.matmul(h1_ps[:, :], w1_hi[:, k, :], lo[:, t.ring(PAIR), :], start=(k == 0), stop=False)
                    pe.matmul(h1_ps[:, :], w1_hi[:, k, :], hi[:, t.ring(PAIR), :], start=False, stop=False)
                    last = pe.matmul(h1_ps[:, :], w1_lo[:, k, :], hi[:, t.ring(PAIR), :], start=False, stop=(k == 1))
                last.then_inc(s_h1ps, 1)

            def layer2(t):
                if not there(t):
                    return
                pe.wait_ge(s_h1, t.g + 1)
                wait_count(pe, s_h2, t.g)
                pe.matmul(h2_ps[:, :], w2s[:, :], h1[:, t.ring(PAIR), :], start=True, stop=True).then_inc(s_h2ps, 1)

            def layer3(t):
                if not there(t):
                    return
                pe.wait_ge(s_h2, t.g + 1)
                wait_count(pe, s_scaled, t.g - t.depth(PAIR) + 1)
                y = y_ps[t.ring(PAIR)]
                pe.matmul(y[:, :].rearrange("p (r f) -> p r f", r=ROWS), ones_bf[:, :],
                          b3rows[:, :].unsqueeze(1).to_broadcast([3, ROWS, P]), start=True, stop=False,
                          skip_group_check=True)
                for r in range(ROWS):
                    last = pe.matmul(y[:, r * P:(r + 1) * P], h2[:, t.ring(PAIR), r * P:(r + 1) * P], w3c[:, :],
                                     start=False, stop=(r == ROWS - 1), skip_group_check=True)
                last.then_inc(s_yps, 1)

            def fast():
                turn_dst()

                def turn(at):
                    layer1(at(0))
                    turn_x(at(1))
                    sum_windows(at(1))
                    layer2(at(0))
                    layer3(at(-1))
                all_turns(pe, turn)

            def general():
                pe.sem_inc(s_gmm, GEN_EDGE_BUFS)

                def sum_all(t):
                    wait_count(pe, s_agglo, t.g)
                    pe.matmul(agg_ps[0][:, :], zeros[:, 0:P], zeros[:, :], start=True, stop=False)
                    with pe.Fori(0, GEN_BATCHES // GEN_EDGE_BUFS) as k:
                        for b in range(GEN_EDGE_BUFS):
                            nth = pe.snap(t.g * (GEN_BATCHES // GEN_EDGE_BUFS) + k)
                            pe.wait_ge(s_ge[b], (nth + 1) * 16)
                            pe.wait_ge(s_ghot, nth * GEN_EDGE_BUFS + b + 1)
                            for c in range(GEN_COLS):
                                last = pe.matmul(agg_ps[0][:, :], gen_edges[:, b, c, :], gen_hot[:, b % PAIR, c, :],
                                                 start=False, stop=False)
                            last.then_inc(s_gmm, 1)
                    pe.matmul(agg_ps[0][:, :], zeros[:, 0:P], zeros[:, :], start=False, stop=True) \
                        .then_inc(s_aggps, 1)

                def turn(t):
                    for stage in (turn_x, sum_all, layer1, layer2, layer3):
                        stage(t)
                general_turns(pe, turn)

            two_paths(pe, fast, general)


_INS = ["x", "dst", "edge_attr_128", "L0_gnn_W1", "L0_gnn_b1", "L0_gnn_W2", "L0_gnn_b2", "L0_gnn_W3", "L0_gnn_b3",
        "L0_gnn_ln_gamma", "L0_gnn_ln_beta"]


def kernel(**inputs):
    import numpy as _np
    import concourse.bacc as _bacc
    from concourse import mybir as _mybir
    from concourse.bass_utils import run_bass_kernel_spmd as _run

    nc = _bacc.Bacc("TRN2", target_bir_lowering=False, num_devices=1)
    arrays, args = {}, []
    for name in _INS:
        a = _np.ascontiguousarray(inputs[name])
        arrays[f"in_{name}_dram"] = a
        args.append(nc.dram_tensor(f"in_{name}_dram", a.shape, _mybir.dt.from_np(a.dtype), kind="ExternalInput").ap())
    shape = _np.shape(inputs["x"])
    args.append(nc.dram_tensor("out_0_dram", shape, _mybir.dt.from_np(_np.dtype("float32")),
                               kind="ExternalOutput").ap())
    gnn_layer(nc, *args)
    r = _run(nc, [arrays], core_ids=[0])
    return r.results[0]["out_0_dram"]
```

```python
from contextlib import ExitStack

import concourse.bass as bass
from concourse import mybir

P = 128
ALU = mybir.AluOpType
ACT = mybir.ActivationFunctionType
AX_X = mybir.AxisListType.X
F32 = mybir.dt.float32
BF16 = mybir.dt.bfloat16
I32 = mybir.dt.int32
F32R = mybir.dt.float32r

ROWS = 4
GROUP = P * ROWS
WIN_NODES = 64
WINS = GROUP // WIN_NODES
BLOCK = 16
EPS = 1e-5

UNROLL = 4
ACT_ROWS = 2
X_BUFS = 4
EDGE_BUFS = 4
OUT_BUFS = 4
PAIR = 2
KEEP = 8
LOOP_FROM = 6
LOAD_X_AHEAD = 5
LOAD_E_AHEAD = 4

GEN_COLS = 10
GEN_EDGE_BUFS = 4


class Turn:

    def __init__(self, g, phase=None, whole=None, general=False):
        self.g, self.phase, self.whole, self.general = g, phase, whole, general

    def ring(self, n):
        return 0 if self.general else self.phase % n

    def round(self, n):
        if self.general:
            return self.g
        return self.whole * (UNROLL // n) + self.phase // n

    def depth(self, n):
        return 1 if self.general else n


def wait_count(eng, sem, value):
    if isinstance(value, int) and value <= 0:
        return
    eng.wait_ge(sem, value)


def gnn_layer(nc, x, dst, edge, w1_dram, b1, w2, b2, w3, b3, gamma, beta, out):
    N, D = x.shape
    E = edge.shape[0]
    assert D == P and N % ROWS == 0 and E % BLOCK == 0
    GROUPS = -(-N // GROUP)
    LAST = GROUPS - 1
    LAST_BASE = N - GROUP
    LAST_SKIP = (LAST * GROUP - LAST_BASE) // ROWS
    DST_PARTS = 125
    RUN = E // DST_PARTS
    RUN_BLOCKS = RUN // BLOCK
    assert E % DST_PARTS == 0 and RUN % BLOCK == 0 and GROUPS <= P
    assert N <= 1 << 16 and RUN_BLOCKS < 1 << 8
    LAST_BLOCK = (E - P) // BLOCK
    TABLE = LAST_BLOCK + 1
    BOUNDS = WINS + 1
    SPAN = P // BLOCK
    GEN_BATCHES = RUN // GEN_COLS
    assert RUN % GEN_COLS == 0 and GEN_BATCHES % GEN_EDGE_BUFS == 0
    LOOP_TURNS = (LAST - LOAD_X_AHEAD - LOOP_FROM) // UNROLL * UNROLL
    LOOP_TO = LOOP_FROM + LOOP_TURNS

    x_rows = x.rearrange("(q r) f -> q (r f)", r=ROWS)
    dst_runs = dst.rearrange("(q j) -> q j", j=RUN)
    edge_runs = edge.rearrange("(q j) f -> q (j f)", j=RUN)
    dst_table = nc.dram_tensor("dst_table", [TABLE, P], I32, kind="Internal").ap()

    with ExitStack() as ctx:
        def sb(name, shape, dt=F32):
            return ctx.enter_context(nc.sbuf_tensor(name, shape, dt))

        def ps(name, shape=(P, GROUP), dt=F32):
            return ctx.enter_context(nc.psum_tensor(name, list(shape), dt))

        def sem(name):
            return ctx.enter_context(nc.semaphore(name))

        w1 = sb("w1", [P, 2, P])
        w1_hi = sb("w1_hi", [P, 2, P], F32R)
        w1_lo = sb("w1_lo", [P, 2, P], F32R)
        w2s = sb("w2s", [P, P])
        w3s = sb("w3s", [P, P])
        w3c = sb("w3c", [P, P])
        w3mean = sb("w3mean", [P, 1])
        b1c = sb("b1c", [P, 1])
        b2c = sb("b2c", [P, 1])
        b3_all = sb("b3_all", [P, P])
        b3mean = sb("b3mean", [P, 1])
        b3c = sb("b3c", [P, P])
        gamma_all = sb("gamma_all", [P, P])
        beta_all = sb("beta_all", [P, P])
        eps_col = sb("eps_col", [P, 1])
        act_scratch = sb("act_scratch", [P, 1])
        ones_col = sb("ones_col", [P, 1])
        zeros_bf = sb("zeros_bf", [P, GROUP], BF16)
        run_blocks_col = sb("run_blocks_col", [P, 1], BF16)
        ones_bf_col = sb("ones_bf_col", [P, 1], BF16)
        ident = sb("ident", [P, P])
        local_node = sb("local_node", [P, ROWS, WIN_NODES // ROWS])

        dst_i = sb("dst_i", [DST_PARTS, RUN], I32)
        dst_f = sb("dst_f", [DST_PARTS, RUN])
        next_i = sb("next_i", [DST_PARTS, 1], I32)
        first_f = sb("first_f", [DST_PARTS, 1])
        next_f = sb("next_f", [DST_PARTS, 1])
        bound_row = sb("bound_row", [DST_PARTS, GROUPS, BOUNDS])
        block_hi = sb("block_hi", [DST_PARTS, RUN_BLOCKS], BF16)
        block_lo = sb("block_lo", [DST_PARTS, RUN_BLOCKS], BF16)
        past_first = sb("past_first", [DST_PARTS, GROUPS, BOUNDS], BF16)
        run_pick = sb("run_pick", [DST_PARTS, GROUPS, BOUNDS], BF16)
        past_block = sb("past_block", [RUN_BLOCKS, GROUPS, BOUNDS], BF16)
        start_f = sb("start_f", [1, GROUPS, WINS])
        start_i = sb("start_i", [1, GROUPS, WINS], I32)
        block_f = sb("block_f", [GROUPS, WINS])
        block_clamped = sb("block_clamped", [GROUPS, WINS])
        block_i = sb("block_i", [GROUPS, WINS], I32)
        base_col = sb("base_col", [GROUPS, 1])
        bound_step = sb("bound_step", [GROUPS, WINS])
        bound_col = sb("bound_col", [GROUPS, WINS])
        too_far = sb("too_far", [GROUPS, WINS])
        falls = sb("falls", [DST_PARTS, RUN])
        bad = sb("bad", [P, 2])
        bad_i = sb("bad_i", [1, 1], I32)
        bad_f = sb("bad_f", [1, 1])
        dst_win = sb("dst_win", [GROUPS, WINS, P], I32)
        dst_rel = sb("dst_rel", [GROUPS, WINS, P])
        dst_loc = sb("dst_loc", [P, GROUPS, WINS])

        x_in = sb("x_in", [P, X_BUFS, GROUP])
        x_keep = sb("x_keep", [P, KEEP, GROUP])
        edges = sb("edges", [P, EDGE_BUFS, WINS, P])
        stats = sb("stats", [P, PAIR, ROWS, 6])
        mean_var = sb("mean_var", [P, PAIR, ROWS, 2])
        std1 = sb("std1", [P, PAIR, ROWS])
        rstd1 = sb("rstd1", [P, PAIR, ROWS])
        x_hat = sb("x_hat", [P, PAIR, ROWS, P])
        one_hot = sb("one_hot", [P, PAIR, WINS, WIN_NODES])
        neg_mean = sb("neg_mean", [P, PAIR, ACT_ROWS])
        x_hi = sb("x_hi", [P, PAIR, GROUP], F32R)
        x_lo = sb("x_lo", [P, PAIR, GROUP], F32R)
        agg_hi = sb("agg_hi", [P, PAIR, GROUP], F32R)
        agg_lo = sb("agg_lo", [P, PAIR, GROUP], F32R)
        h1 = sb("h1", [P, PAIR, GROUP])
        h2 = sb("h2", [P, PAIR, GROUP])
        squares = sb("squares", [P, ROWS, P])
        sum_sq = sb("sum_sq", [P, PAIR, ROWS])
        std2 = sb("std2", [P, PAIR, ROWS])
        rstd2 = sb("rstd2", [P, PAIR, ROWS])
        result = sb("result", [P, OUT_BUFS, ROWS, P])

        gen_edges = sb("gen_edges", [DST_PARTS, GEN_EDGE_BUFS, GEN_COLS, P])
        gen_hot = sb("gen_hot", [DST_PARTS, PAIR, GEN_COLS, GROUP])
        gen_rel = sb("gen_rel", [DST_PARTS, RUN])
        group_node = sb("group_node", [DST_PARTS, WINS, ROWS, WIN_NODES // ROWS])
        zeros = sb("zeros", [P, GROUP])

        x_ps = [ps(f"x_ps{i}") for i in range(PAIR)]
        agg_ps = [ps(f"agg_ps{i}") for i in range(PAIR)]
        h1_ps = ps("h1_ps")
        h2_ps = ps("h2_ps")
        y_ps = [ps(f"y_ps{i}") for i in range(PAIR)]

        s_dst = sem("dst_loaded")
        s_next = sem("next_loaded")
        s_table = sem("table_written")
        s_weights = sem("weights_loaded")
        s_consts = sem("consts_made")
        s_iota = sem("bounds_made")
        s_ident0 = sem("ident_cleared")
        s_prep = sem("weights_prepared")
        s_split = sem("w1_split")
        s_ix = sem("index_steps")
        s_pick = sem("blocks_picked")
        s_rank = sem("ranks_counted")
        s_win = [sem(f"dst_windows_loaded{i}") for i in range(2)]
        s_rel = sem("dst_rel_ready")
        s_turned = sem("dst_turned")
        s_badsum = sem("bad_summed")

        s_x = [sem(f"x_loaded{i}") for i in range(X_BUFS)]
        s_e = [sem(f"edges_loaded{i}") for i in range(EDGE_BUFS)]
        s_stored = [sem(f"stored{i}") for i in range(OUT_BUFS)]
        s_last_stored = sem("last_group_stored")
        s_stats = sem("stats_ready")
        s_var = sem("var_ready")
        s_std1 = sem("std1_ready")
        s_rstd1 = sem("rstd1_ready")
        s_hat = sem("x_hat_ready")
        s_keep = sem("x_keep_ready")
        s_hot = sem("one_hot_ready")
        s_xps = sem("x_ps_ready")
        s_aggps = sem("agg_ps_ready")
        s_hat_act = sem("x_hat_rows_ready")
        s_nmean = sem("neg_mean_ready")
        s_xhi = sem("x_hi_ready")
        s_xlo = sem("x_lo_ready")
        s_agghi = sem("agg_hi_ready")
        s_agglo = sem("agg_lo_ready")
        s_h1ps = sem("h1_ps_ready")
        s_h1 = sem("h1_ready")
        s_h2ps = sem("h2_ps_ready")
        s_h2 = sem("h2_ready")
        s_owned = sem("y_ps_owned")
        s_biased = sem("y_ps_holds_b3")
        s_yps = sem("y_ps_ready")
        s_sq = sem("sum_sq_ready")
        s_std2 = sem("std2_ready")
        s_rstd2 = sem("rstd2_ready")
        s_scaled = sem("scaled_ready")
        s_out = sem("out_ready")

        s_ge = [sem(f"gen_edges_loaded{i}") for i in range(GEN_EDGE_BUFS)]
        s_ghot = sem("gen_hot_ready")
        s_gmm = sem("gen_batches_summed")
        s_grel = sem("gen_rel_steps")

        WEIGHT_LOADS = 9
        HALF = GROUPS // 2
        assert GROUPS % 2 == 0 and HALF * BOUNDS <= 512

        def all_turns(eng, turn):
            for i in range(-LOAD_E_AHEAD, LOOP_FROM):
                turn(lambda ahead, i=i: Turn(i + ahead, i + ahead, 0))
            with eng.Fori(0, LOOP_TURNS // UNROLL) as j:
                first = eng.snap(j * UNROLL)
                for u in range(UNROLL):
                    phase = LOOP_FROM + u
                    turn(lambda ahead, u=u, phase=phase: Turn(first + (phase + ahead), phase + ahead, j))
            for i in range(LOOP_TO, GROUPS + 4):
                turn(lambda ahead, i=i: Turn(i + ahead, i + ahead, 0))

        def there(t):
            return not isinstance(t.g, int) or 0 <= t.g < GROUPS

        def is_first(t):
            return isinstance(t.g, int) and t.g == 0

        def is_preloaded(t):
            return isinstance(t.g, int) and t.g < (1 if t.general else X_BUFS)

        def is_last(t):
            return isinstance(t.g, int) and t.g == LAST

        def kept(t):
            slot = t.g % KEEP if isinstance(t.g, int) else t.g & (KEEP - 1)
            if t.general:
                slot = 0
            return x_keep[:, bass.ds(slot, 1), :].rearrange("p o (r f) -> p (o r) f", r=ROWS)

        def add_kept(eng, t):
            eng.wait_ge(s_scaled, t.g + 1)
            eng.wait_ge(s_keep, t.g + 1)
            r = result[:, t.ring(OUT_BUFS), :, :]
            eng.tensor_tensor(r, r, kept(t), ALU.add).then_inc(s_out, 1)

        def store_result(eng, t, signal):
            skip = LAST_SKIP if is_last(t) else 0
            node = LAST_BASE + skip * ROWS if is_last(t) else t.g * GROUP
            eng.dma_start(out[bass.ds(node, GROUP - skip * ROWS), :].rearrange("(p r) f -> p (r f)", r=ROWS),
                          result[skip:P, t.ring(OUT_BUFS), :, :].rearrange("p r f -> p (r f)")) \
                .then_inc(signal, 16)

        def by_window(ap):
            return ap.rearrange("p (r w c) -> p w r c", r=ROWS, w=WINS)

        def sums(t):
            return agg_ps[t.ring(PAIR)][:, :].rearrange("p (w r c) -> p w r c", r=ROWS, w=WINS)

        def two_paths(eng, fast, general):
            eng.wait_ge(s_ix, IX_DONE)
            flag = eng.value_load(bad_i[0:1, 0:1], min_val=0, max_val=2 * P)
            with eng.If(flag < 1):
                fast()
            with eng.Else():
                general()

        def general_turns(eng, turn):
            turn(Turn(0, general=True))
            with eng.Fori(1, LAST) as g:
                turn(Turn(g, general=True))
            turn(Turn(LAST, general=True))

        IX_DONE = 17
        BLOCKS_FOUND = 12
        PREPARED = 6

        block = ctx.enter_context(nc.Block())

        @block.sync
        def _(sp):
            sp.dma_start(dst_i[:, :], dst_runs).then_inc(s_dst, 16)
            with nc.allow_non_contiguous_dma("one first dst of each run"):
                sp.dma_start(next_i[0:DST_PARTS - 1, :], dst_runs[1:DST_PARTS, 0:1]).then_inc(s_next, 16)
            rows = TABLE // 16 * 16
            for r0, r1 in ((0, rows), (rows, TABLE)):
                src = bass.AP(dst.tensor, BLOCK * r0, [[BLOCK, r1 - r0], [1, P]])
                sp.dma_start(dst_table[r0:r1, :], src).then_inc(s_table, 16)
            for tile, src in ((w1[:, 0, :], w1_dram[0:P, :]), (w1[:, 1, :], w1_dram[P:2 * P, :]),
                              (w2s[:, :], w2), (w3s[:, :], w3)):
                sp.dma_start(tile, src).then_inc(s_weights, 16)
            with nc.allow_non_contiguous_dma("a bias is a column"):
                for tile, src in ((b1c, b1), (b2c, b2)):
                    sp.dma_start(tile[:, :], src.rearrange("(p o) -> p o", o=1)).then_inc(s_weights, 16)
            for tile, src in ((b3_all, b3), (gamma_all, gamma), (beta_all, beta)):
                sp.dma_start(tile[:, :], bass.AP(src.tensor, 0, [[0, P], [1, P]])).then_inc(s_weights, 16)
            def load_edges(t):
                if not there(t):
                    return
                wait_count(sp, s_aggps, t.g - EDGE_BUFS + 1)
                _, starts = nc.values_load_multi_w_load_instructions(
                    start_i[0:1, bass.ds(t.g, 1), :].rearrange("o g w -> o (g w)"), engines=[sp.engine],
                    min_val=0, max_val=E - P, skip_runtime_bounds_check_because="the index stage keeps starts within 0 and E - P")
                for w in range(WINS):
                    sp.dma_start(edges[:, t.ring(EDGE_BUFS), w, :], edge[bass.ds(starts[w], P), :]) \
                        .then_inc(s_e[t.ring(EDGE_BUFS)], 16)

            def fast():
                def turn(at):
                    load_edges(at(LOAD_E_AHEAD))
                    if is_last(at(-2)):
                        sp.wait_ge(s_out, LAST + 1)
                        store_result(sp, at(-2), s_last_stored)
                        sp.wait_ge(s_last_stored, 16)
                all_turns(sp, turn)

            def general():
                def turn(t):
                    with sp.Fori(0, GEN_BATCHES // GEN_EDGE_BUFS) as k:
                        for b in range(GEN_EDGE_BUFS):
                            sp.wait_ge(s_gmm, t.g * GEN_BATCHES + k * GEN_EDGE_BUFS + (b + 1))
                            sp.dma_start(gen_edges[:, b, :, :].rearrange("p c f -> p (c f)"),
                                         edge_runs[:, bass.ds((k * GEN_EDGE_BUFS + b) * GEN_COLS * P, GEN_COLS * P)]) \
                                .then_inc(s_ge[b], 16)
                general_turns(sp, turn)

            two_paths(sp, fast, general)

        @block.gpsimd
        def _(pool):
            pool.iota(bound_row[:, 0:LAST, :], [[GROUP, LAST], [WIN_NODES, BOUNDS]], base=0,
                      channel_multiplier=0, allow_small_or_imprecise_dtypes=True)
            pool.iota(bound_row[:, LAST:GROUPS, :], [[0, 1], [WIN_NODES, BOUNDS]], base=LAST_BASE,
                      channel_multiplier=0, allow_small_or_imprecise_dtypes=True).then_inc(s_iota, 1)
            pool.memset(ident[:, :], 0.0).then_inc(s_ident0, 1)
            pool.wait_ge(s_ident0, 1)
            pool.affine_select(out=ident[:, :], in_=ident[:, :], compare_op=ALU.not_equal, fill=1.0,
                               base=0, pattern=[[-1, P]], channel_multiplier=1)
            pool.iota(base_col[:, :], [[0, 1]], base=0, channel_multiplier=GROUP,
                      allow_small_or_imprecise_dtypes=True)
            pool.iota(bound_step[:, :], [[WIN_NODES, WINS]], base=0, channel_multiplier=0,
                      allow_small_or_imprecise_dtypes=True)
            pool.iota(local_node[:, :, :], [[1, ROWS], [ROWS, WIN_NODES // ROWS]], base=0,
                      channel_multiplier=0, allow_small_or_imprecise_dtypes=True)
            pool.iota(group_node[:, :, :, :], [[WIN_NODES, WINS], [1, ROWS], [ROWS, WIN_NODES // ROWS]], base=0,
                      channel_multiplier=0, allow_small_or_imprecise_dtypes=True).then_inc(s_consts, 1)
            for g in range(X_BUFS):
                pool.dma_start(x_in[:, g, :], x_rows[g * P:(g + 1) * P, :]).then_inc(s_x[g], 16)
            pool.wait_ge(s_table, 32)
            pool.wait_ge(s_ix, BLOCKS_FOUND)
            for w in range(WINS):
                pool.indirect_dma_start(
                    out=dst_win[:, w, :], out_offset=None, in_=dst_table[:, :],
                    in_offset=bass.IndirectOffsetOnAxis(ap=block_i[:, w:w + 1], axis=0)) \
                    .then_inc(s_win[w // 4], 16)
            for half in range(2):
                pool.wait_ge(s_win[half], 16 * 4)
            pool.wait_ge(s_weights, 16 * WEIGHT_LOADS)

            def wait_for_slot(t):
                if not there(t) or is_preloaded(t):
                    return
                wait_count(pool, s_hat, t.g - t.depth(X_BUFS) + 1)
                wait_count(pool, s_hat_act, t.g - t.depth(X_BUFS) + 1)
                wait_count(pool, s_keep, t.g - t.depth(X_BUFS) + 1)

            def load_x(t):
                if not there(t) or is_preloaded(t):
                    return
                row = LAST_BASE // ROWS if is_last(t) else t.g * P
                pool.dma_start(x_in[:, t.ring(X_BUFS), :], x_rows[bass.ds(row, P), :]) \
                    .then_inc(s_x[t.ring(X_BUFS)], 16)

            def keep_x(t):
                if not there(t):
                    return
                pool.wait_ge(s_x[t.ring(X_BUFS)], (t.round(X_BUFS) + 1) * 16)
                wait_count(pool, s_out, t.g - t.depth(KEEP) + 1)
                pool.tensor_tensor(kept(t), x_in[:, t.ring(X_BUFS), :].rearrange("p (r f) -> p r f", r=ROWS),
                                   beta_all[:, :].unsqueeze(1).to_broadcast([P, ROWS, P]), ALU.add) \
                    .then_inc(s_keep, 1)

            def store(t):
                pool.wait_ge(s_out, t.g + 1)
                store_result(pool, t, s_stored[t.ring(OUT_BUFS)])

            def add_and_store(t):
                if not there(t):
                    return
                add_kept(pool, t)
                store(t)

            def fast():
                def turn(at):
                    wait_for_slot(at(LOAD_X_AHEAD))
                    keep_x(at(3))
                    load_x(at(LOAD_X_AHEAD))
                    if not is_last(at(-2)):
                        add_and_store(at(-2))
                all_turns(pool, turn)
                for i in range(OUT_BUFS):
                    pool.wait_ge(s_stored[i], 16 * len(range(i, LAST, OUT_BUFS)))

            def general():
                def turn(t):
                    load_x(t)
                    keep_x(t)
                    add_and_store(t)
                general_turns(pool, turn)
                pool.wait_ge(s_stored[0], 16 * GROUPS)

            two_paths(pool, fast, general)

        @block.scalar
        def _(act):
            act.wait_ge(s_ix, 1)
            act.activation(act_scratch[:, :], eps_col[:, :], ACT.Sqrt)
            act.wait_ge(s_prep, PREPARED)
            act.wait_ge(s_weights, 16 * WEIGHT_LOADS)

            def std_x(t):
                if not there(t):
                    return
                act.wait_ge(s_var, t.g + 1)
                wait_count(act, s_rstd1, t.g - t.depth(PAIR) + 1)
                act.activation(std1[:, t.ring(PAIR), :], mean_var[:, t.ring(PAIR), :, 1], ACT.Sqrt,
                               bias=eps_col[:, :]).then_inc(s_std1, 1)

            def normalise_rows(t):
                if not there(t):
                    return
                act.wait_ge(s_nmean, t.g + 1)
                wait_count(act, s_xps, t.g - t.depth(PAIR) + 1)
                for r in range(ACT_ROWS):
                    last = act.activation(x_hat[:, t.ring(PAIR), r, :],
                                          x_in[:, t.ring(X_BUFS), r * P:(r + 1) * P], ACT.Identity,
                                          bias=neg_mean[:, t.ring(PAIR), r:r + 1],
                                          scale=rstd1[:, t.ring(PAIR), r:r + 1])
                last.then_inc(s_hat_act, 1)

            def relu_x(t):
                if not there(t):
                    return
                act.wait_ge(s_xps, t.g + 1)
                wait_count(act, s_h1ps, t.g - t.depth(PAIR) + 1)
                act.activation(x_hi[:, t.ring(PAIR), :], x_ps[t.ring(PAIR)][:, :], ACT.Relu).then_inc(s_xhi, 1)

            def copy_agg(t):
                if not there(t):
                    return
                act.wait_ge(s_aggps, t.g + 1)
                wait_count(act, s_h1ps, t.g - t.depth(PAIR) + 1)
                act.activation(by_window(agg_hi[:, t.ring(PAIR), :]), sums(t), ACT.Copy).then_inc(s_agghi, 1)

            def relu_h1(t):
                if not there(t):
                    return
                act.wait_ge(s_h1ps, t.g + 1)
                wait_count(act, s_h2ps, t.g - t.depth(PAIR) + 1)
                act.activation(h1[:, t.ring(PAIR), :], h1_ps[:, :], ACT.Relu, bias=b1c[:, :]).then_inc(s_h1, 1)

            def relu_h2(t):
                if not there(t):
                    return
                act.wait_ge(s_h2ps, t.g + 1)
                wait_count(act, s_yps, t.g - t.depth(PAIR) + 1)
                act.activation(h2[:, t.ring(PAIR), :], h2_ps[:, :], ACT.Relu, bias=b2c[:, :]).then_inc(s_h2, 1)

            def place_b3(t):
                if not there(t):
                    return
                act.wait_ge(s_owned, 1)
                wait_count(act, s_scaled, t.g - t.depth(PAIR) + 1)
                act.activation(y_ps[t.ring(PAIR)][:, :].rearrange("p (r f) -> p r f", r=ROWS),
                               b3c[:, :].unsqueeze(1).to_broadcast([P, ROWS, P]), ACT.Copy).then_inc(s_biased, 1)

            def sum_squares(t):
                if not there(t):
                    return
                act.wait_ge(s_yps, t.g + 1)
                for r in range(ROWS):
                    last = act.activation(squares[:, r, :], y_ps[t.ring(PAIR)][:, r * P:(r + 1) * P], ACT.Square,
                                          accum_out=sum_sq[:, t.ring(PAIR), r:r + 1])
                last.then_inc(s_sq, 1)

            def std_y(t):
                if not there(t):
                    return
                act.wait_ge(s_sq, t.g + 1)
                wait_count(act, s_rstd2, t.g - t.depth(PAIR) + 1)
                act.activation(std2[:, t.ring(PAIR), :], sum_sq[:, t.ring(PAIR), :], ACT.Sqrt,
                               bias=eps_col[:, :], scale=1.0 / D).then_inc(s_std2, 1)

            def fast():
                def turn(at):
                    ending = isinstance(at(0).g, int) and at(0).g >= LAST
                    if ending:
                        place_b3(at(-1))
                    sum_squares(at(-2))
                    std_y(at(-2))
                    relu_h1(at(0))
                    relu_x(at(1))
                    if not ending:
                        place_b3(at(-1))
                    copy_agg(at(1))
                    std_x(at(3))
                    normalise_rows(at(2))
                    relu_h2(at(0))
                all_turns(act, turn)

            def general():
                def turn(t):
                    for stage in (std_x, normalise_rows, relu_x, copy_agg, relu_h1, relu_h2, place_b3, sum_squares, std_y):
                        stage(t)
                general_turns(act, turn)

            two_paths(act, fast, general)

        @block.vector
        def _(dve):
            steps = [0]

            def step(ins):
                steps[0] += 1
                ins.then_inc(s_ix, 1)
                dve.wait_ge(s_ix, steps[0])

            def half_of(ap, half):
                return ap[:, half * HALF:(half + 1) * HALF, :]

            dve.memset(ones_col[:, :], 1.0)
            dve.memset(ones_bf_col[:, :], 1.0)
            dve.memset(run_blocks_col[:, :], float(RUN_BLOCKS))
            dve.memset(bad[:, :], 0.0)
            dve.memset(eps_col[:, :], EPS)
            dve.memset(zeros[:, :], 0.0)
            dve.memset(zeros_bf[:, :], 0.0)
            step(dve.memset(next_f[:, :], float(N)))
            dve.wait_ge(s_dst, 16)
            dve.wait_ge(s_next, 16)
            dve.tensor_copy(next_f[0:DST_PARTS - 1, :], next_i[0:DST_PARTS - 1, :])
            dve.tensor_copy(block_hi[:, :], dst_i[:, 0:RUN:BLOCK])
            dve.tensor_copy(first_f[:, :], dst_i[:, 0:1])
            step(dve.tensor_copy(dst_f[:, :], dst_i[:, :]))
            dve.tensor_tensor(block_lo[:, :], dst_f[:, 0:RUN:BLOCK], block_hi[:, :], ALU.subtract)
            step(dve.memset(first_f[0:1, :], -1.0))
            dve.wait_ge(s_iota, 1)
            for half in range(2):
                step(dve.tensor_scalar(half_of(past_first, half), half_of(bound_row, half), first_f[:, 0:1], None,
                                       ALU.is_gt))
                step(dve.scalar_tensor_tensor(out=half_of(run_pick, half), in0=half_of(bound_row, half),
                                              scalar=next_f[:, 0:1], in1=half_of(past_first, half),
                                              op0=ALU.is_le, op1=ALU.mult))
            assert steps[0] == 7
            for half in range(2):
                dve.wait_ge(s_pick, half + 1)
                last = dve.tensor_tensor(
                    half_of(past_block, half),
                    x_ps[half][0:RUN_BLOCKS, 0:HALF * BOUNDS].rearrange("p (g b) -> p g b", b=BOUNDS),
                    half_of(bound_row, half)[0:RUN_BLOCKS], ALU.is_lt)
            step(last)
            assert steps[0] == 8
            dve.tensor_tensor(falls[:, RUN - 1:RUN], dst_f[:, RUN - 1:RUN], next_f[:, :], ALU.is_gt)
            step(dve.tensor_tensor(falls[:, 0:RUN - 1], dst_f[:, 0:RUN - 1], dst_f[:, 1:RUN], ALU.is_gt))
            step(dve.tensor_reduce(bad[0:DST_PARTS, 1:2], falls[:, :], AX_X, ALU.max))
            dve.wait_ge(s_rank, 1)
            step(dve.tensor_scalar(block_f[:, :], agg_ps[0][0:GROUPS, 0:BOUNDS][:, 0:WINS], -float(RUN_BLOCKS + 1),
                                   0.0, ALU.add, ALU.max))
            step(dve.tensor_scalar(block_i[:, :], block_f[:, :], float(LAST_BLOCK), None, ALU.min))
            assert steps[0] == BLOCKS_FOUND
            step(dve.tensor_scalar(block_clamped[:, :], block_f[:, :], float(LAST_BLOCK), None, ALU.min))
            step(dve.scalar_tensor_tensor(out=too_far[:, :], in0=agg_ps[0][0:GROUPS, 1:BOUNDS],
                                          scalar=-(SPAN + RUN_BLOCKS + 0.5), in1=block_clamped[:, :],
                                          op0=ALU.add, op1=ALU.is_gt))
            dve.tensor_reduce(bad[0:GROUPS, 0:1], too_far[:, :], AX_X, ALU.max)
            dve.wait_ge(s_rank, 2)
            for half in range(2):
                rows = (h1_ps, h2_ps)[half][0:1, 0:HALF * BOUNDS].rearrange("p (g b) -> p g b", b=BOUNDS)
                last = dve.tensor_scalar(half_of(start_f, half), rows[:, :, 0:WINS],
                                         -float(RUN_BLOCKS + 1), 0.0, ALU.add, ALU.max)
            step(last)
            step(dve.tensor_scalar(start_i[:, :, :], start_f[:, :, :], float(LAST_BLOCK), float(BLOCK),
                                   ALU.min, ALU.mult))
            assert steps[0] == IX_DONE - 1
            dve.wait_ge(s_badsum, 1)
            dve.tensor_reduce(bad_f[:, :], agg_ps[1][0:1, 0:2], AX_X, ALU.add).then_inc(s_prep, 1)
            dve.wait_ge(s_prep, 1)
            step(dve.tensor_copy(bad_i[:, :], bad_f[:, :]))
            assert steps[0] == IX_DONE

            dve.wait_ge(s_weights, 16 * WEIGHT_LOADS)
            dve.tensor_reduce(b3mean[:, :], b3_all[:, :], AX_X, ALU.add)
            dve.tensor_reduce(w3mean[:, :], w3s[:, :], AX_X, ALU.add).then_inc(s_prep, 1)
            dve.wait_ge(s_prep, 2)
            dve.tensor_scalar(b3mean[:, :], b3mean[:, :], 1.0 / D, None, ALU.mult)
            dve.tensor_scalar(w3mean[:, :], w3mean[:, :], 1.0 / D, None, ALU.mult).then_inc(s_prep, 1)
            dve.wait_ge(s_prep, 3)
            dve.tensor_scalar(w3c[:, :], w3s[:, :], w3mean[:, 0:1], None, ALU.subtract)
            dve.tensor_scalar(b3c[:, :], b3_all[:, :], b3mean[:, 0:1], None, ALU.subtract).then_inc(s_prep, 1)

            dve.tensor_copy(w1_hi[:, :, :], w1[:, :, :]).then_inc(s_split, 1)
            dve.wait_ge(s_split, 1)
            dve.tensor_tensor(w1_lo[:, :, :], w1[:, :, :], w1_hi[:, :, :].bitcast(F32), ALU.subtract) \
                .then_inc(s_split, 1)

            dve.wait_ge(s_consts, 1)
            dve.tensor_scalar(base_col[:, :], base_col[:, :], float(LAST_BASE), None, ALU.min).then_inc(s_prep, 1)
            dve.wait_ge(s_prep, 5)
            dve.tensor_scalar(bound_col[:, :], bound_step[:, :], base_col[:, 0:1], None, ALU.add).then_inc(s_prep, 1)
            dve.wait_ge(s_prep, PREPARED)

            def subtract_bounds(half):
                wins = slice(half * 4, half * 4 + 4)
                dve.wait_ge(s_win[half], 16 * 4)
                dve.tensor_tensor(dst_rel[:, wins, :], dst_win[:, wins, :],
                                  bound_col[:, wins].unsqueeze(2).to_broadcast([GROUPS, 4, P]),
                                  ALU.subtract).then_inc(s_rel, 1)

            def copy_located():
                for half in range(2):
                    dve.wait_ge(s_turned, half + 1)
                    last = dve.tensor_copy(
                        dst_loc[:, :, half * 4:half * 4 + 4].rearrange("p g w -> p w g"),
                        y_ps[half][:, 0:4 * GROUPS].rearrange("p (w g) -> p w g", w=4))
                last.then_inc(s_rel, 1)
                dve.wait_ge(s_rel, 3)

            def x_rows_of(t):
                return x_in[:, t.ring(X_BUFS), :].rearrange("p (r f) -> p r f", r=ROWS)

            def x_stats(t):
                if not there(t):
                    return
                dve.wait_ge(s_x[t.ring(X_BUFS)], (t.round(X_BUFS) + 1) * 16)
                for r in range(ROWS):
                    last = dve.bn_stats(stats[:, t.ring(PAIR), r, :], x_rows_of(t)[:, r, :])
                last.then_inc(s_stats, 1)
                dve.wait_ge(s_stats, t.g + 1)

            def x_mean_var(t):
                if not there(t):
                    return
                for r in range(ROWS):
                    last = dve.bn_aggr(mean_var[:, t.ring(PAIR), r, :], stats[:, t.ring(PAIR), r, :])
                last.then_inc(s_var, 1)

            def reciprocal_x(t):
                if not there(t):
                    return
                dve.wait_ge(s_std1, t.g + 1)
                wait_count(dve, s_hat_act, t.g - t.depth(PAIR) + 1)
                dve.reciprocal(rstd1[:, t.ring(PAIR), :], std1[:, t.ring(PAIR), :]).then_inc(s_rstd1, 1)

            def negative_mean(t):
                if not there(t):
                    return
                dve.wait_ge(s_rstd1, t.g + 1)
                dve.scalar_tensor_tensor(out=neg_mean[:, t.ring(PAIR), :], in0=mean_var[:, t.ring(PAIR), 0:ACT_ROWS, 0],
                                         scalar=-1.0, in1=rstd1[:, t.ring(PAIR), 0:ACT_ROWS],
                                         op0=ALU.mult, op1=ALU.mult).then_inc(s_nmean, 1)

            def normalise(t):
                if not there(t):
                    return
                wait_count(dve, s_xps, t.g - t.depth(PAIR) + 1)
                for r in range(ACT_ROWS, ROWS):
                    last = dve.tensor_scalar(x_hat[:, t.ring(PAIR), r, :], x_rows_of(t)[:, r, :],
                                             mean_var[:, t.ring(PAIR), r, 0:1], rstd1[:, t.ring(PAIR), r:r + 1],
                                             ALU.subtract, ALU.mult)
                last.then_inc(s_hat, 1)

            def low_x(t):
                if not there(t):
                    return
                dve.wait_ge(s_xhi, t.g + 1)
                dve.scalar_tensor_tensor(out=x_lo[:, t.ring(PAIR), :], in0=x_ps[t.ring(PAIR)][:, :], scalar=0.0,
                                         in1=x_hi[:, t.ring(PAIR), :].bitcast(F32), op0=ALU.max,
                                         op1=ALU.subtract).then_inc(s_xlo, 1)

            def low_agg(t):
                if not there(t):
                    return
                dve.wait_ge(s_agghi, t.g + 1)
                dve.tensor_tensor(by_window(agg_lo[:, t.ring(PAIR), :]), sums(t),
                                  by_window(agg_hi[:, t.ring(PAIR), :].bitcast(F32)),
                                  ALU.subtract).then_inc(s_agglo, 1)

            def make_one_hot(t):
                if not there(t):
                    return
                wait_count(dve, s_aggps, t.g - PAIR + 1)
                dve.tensor_tensor(
                    one_hot[:, t.ring(PAIR), :, :],
                    local_node[:, :, :].rearrange("p r c -> p (r c)").unsqueeze(1).to_broadcast([P, WINS, WIN_NODES]),
                    dst_loc[:, bass.ds(t.g, 1), :].rearrange("p o w -> p (o w)").unsqueeze(2)
                    .to_broadcast([P, WINS, WIN_NODES]), ALU.is_equal).then_inc(s_hot, 1)

            def reciprocal_y(t):
                if not there(t):
                    return
                dve.wait_ge(s_std2, t.g + 1)
                dve.reciprocal(rstd2[:, t.ring(PAIR), :], std2[:, t.ring(PAIR), :]).then_inc(s_rstd2, 1)

            def scale_y(t):
                if not there(t):
                    return
                dve.wait_ge(s_rstd2, t.g + 1)
                wait_count(dve, s_stored[t.ring(OUT_BUFS)], t.round(OUT_BUFS) * 16)
                for r in range(ROWS):
                    last = dve.scalar_tensor_tensor(
                        out=result[:, t.ring(OUT_BUFS), r, :], in0=y_ps[t.ring(PAIR)][:, r * P:(r + 1) * P],
                        scalar=rstd2[:, t.ring(PAIR), r:r + 1], in1=gamma_all[:, :], op0=ALU.mult, op1=ALU.mult)
                last.then_inc(s_scaled, 1)

            def fast():
                subtract_bounds(0)

                def turn(at):
                    x_stats(at(3))
                    reciprocal_x(at(2))
                    x_mean_var(at(3))
                    reciprocal_y(at(-2))
                    negative_mean(at(2))
                    scale_y(at(-2))
                    low_x(at(1))
                    low_agg(at(1))
                    normalise(at(2))
                    if is_first(at(2)):
                        subtract_bounds(1)
                        copy_located()
                    make_one_hot(at(2))
                    if is_last(at(-2)):
                        dve.wait_ge(s_out, LAST)
                        add_kept(dve, at(-2))
                all_turns(dve, turn)

            def general():
                dve.tensor_copy(gen_rel[:, :], dst_f[:, :]).then_inc(s_grel, 1)

                def turn(t):
                    x_stats(t)
                    dve.memset(bad_f[:, :], 0.0)
                    x_mean_var(t)
                    reciprocal_x(t)
                    negative_mean(t)
                    normalise(t)
                    low_x(t)
                    dve.wait_ge(s_prep, PREPARED)
                    dve.wait_ge(s_grel, t.g + 1)
                    if is_last(t):
                        dve.tensor_scalar(gen_rel[:, :], gen_rel[:, :], float(LAST * GROUP - LAST_BASE), None,
                                          ALU.add).then_inc(s_grel, 1)
                        dve.wait_ge(s_grel, LAST + 2)
                    with dve.Fori(0, GEN_BATCHES // PAIR) as k:
                        for b in range(PAIR):
                            dve.wait_ge(s_gmm, t.g * GEN_BATCHES + k * PAIR + (b + GEN_EDGE_BUFS - PAIR + 1))
                            for c in range(GEN_COLS):
                                last = dve.tensor_scalar(
                                    gen_hot[:, b, c, :], group_node[:, :, :, :].rearrange("p w r c -> p (w r c)"),
                                    gen_rel[:, bass.ds((k * PAIR + b) * GEN_COLS + c, 1)], None, ALU.is_equal)
                            last.then_inc(s_ghot, 1)
                    if not is_last(t):
                        dve.wait_ge(s_ghot, (t.g + 1) * GEN_BATCHES)
                        dve.tensor_scalar(gen_rel[:, :], gen_rel[:, :], -float(GROUP), None,
                                          ALU.add).then_inc(s_grel, 1)
                    low_agg(t)
                    reciprocal_y(t)
                    scale_y(t)
                general_turns(dve, turn)

            two_paths(dve, fast, general)

        @block.tensor
        def _(pe):
            for half in range(2):
                pick = x_ps[half][0:RUN_BLOCKS, 0:HALF * BOUNDS]
                runs = run_pick[:, half * HALF:(half + 1) * HALF, :].rearrange("p g b -> p (g b)")
                pe.wait_ge(s_ix, (5, 7)[half])
                pe.matmul(pick, block_hi[:, :], runs, start=True, stop=False)
                pe.matmul(pick, block_lo[:, :], runs, start=False, stop=True).then_inc(s_pick, 1)
            pe.wait_ge(s_ix, 8)
            for b in range(BOUNDS):
                pe.matmul(agg_ps[0][0:GROUPS, b:b + 1], past_first[:, :, b], run_blocks_col[0:DST_PARTS, :],
                          start=True, stop=False)
                last = pe.matmul(agg_ps[0][0:GROUPS, b:b + 1], past_block[:, :, b], ones_bf_col[0:RUN_BLOCKS, :],
                                 start=False, stop=True)
            last.then_inc(s_rank, 1)
            for half in range(2):
                part = slice(half * HALF, (half + 1) * HALF)
                row = (h1_ps, h2_ps)[half][0:1, 0:HALF * BOUNDS]
                pe.matmul(row, run_blocks_col[0:DST_PARTS, :], past_first[:, part, :].rearrange("p g b -> p (g b)"),
                          start=True, stop=False)
                last = pe.matmul(row, ones_bf_col[0:RUN_BLOCKS, :], past_block[:, part, :].rearrange("p g b -> p (g b)"),
                                 start=False, stop=True)
            last.then_inc(s_rank, 1)
            pe.wait_ge(s_ix, IX_DONE - 1)
            pe.matmul(agg_ps[1][0:1, 0:2], ones_col[:, :], bad[:, :], start=True, stop=True).then_inc(s_badsum, 1)
            pe.wait_ge(s_consts, 1)

            def keep_clock_up(products):
                for _ in range(products):
                    pe.matmul(h2_ps[0:RUN_BLOCKS, 0:HALF * BOUNDS], block_hi[:, :],
                              run_pick[:, 0:HALF, :].rearrange("p g b -> p (g b)"), start=True, stop=True)

            def wait_for_weights():
                pe.wait_ge(s_prep, PREPARED)
                pe.wait_ge(s_split, 2)
                pe.wait_ge(s_weights, 16 * WEIGHT_LOADS)

            def turn_dst(half):
                pe.wait_ge(s_rel, half + 1)
                for w in range(4):
                    last = pe.transpose(y_ps[half][:, w * GROUPS:(w + 1) * GROUPS], dst_rel[:, half * 4 + w, :],
                                        ident[0:GROUPS, 0:GROUPS])
                last.then_inc(s_turned, 1)

            def own_y_ps():
                for y in y_ps:
                    last = pe.matmul(y[:, :], zeros_bf[:, 0:P], zeros_bf[:, :], start=True, stop=True)
                last.then_inc(s_owned, 1)

            def turn_x(t):
                if not there(t):
                    return
                pe.wait_ge(s_hat, t.g + 1)
                pe.wait_ge(s_hat_act, t.g + 1)
                wait_count(pe, s_xlo, t.g - t.depth(PAIR) + 1)
                for r in range(ROWS):
                    last = pe.transpose(x_ps[t.ring(PAIR)][:, r * P:(r + 1) * P], x_hat[:, t.ring(PAIR), r, :],
                                        ident[:, :])
                last.then_inc(s_xps, 1)

            def sum_windows(t):
                if not there(t):
                    return
                pe.wait_ge(s_hot, t.g + 1)
                pe.wait_ge(s_e[t.ring(EDGE_BUFS)], (t.round(EDGE_BUFS) + 1) * (16 * WINS))
                wait_count(pe, s_agglo, t.g - PAIR + 1)
                for w in range(WINS):
                    last = pe.matmul(agg_ps[t.ring(PAIR)][:, w * WIN_NODES:(w + 1) * WIN_NODES],
                                     edges[:, t.ring(EDGE_BUFS), w, :], one_hot[:, t.ring(PAIR), w, :],
                                     start=True, stop=True)
                last.then_inc(s_aggps, 1)

            def layer1(t):
                if not there(t):
                    return
                pe.wait_ge(s_xlo, t.g + 1)
                pe.wait_ge(s_agglo, t.g + 1)
                wait_count(pe, s_h1, t.g)
                for k, (hi, lo) in enumerate(((x_hi, x_lo), (agg_hi, agg_lo))):
                    pe.matmul(h1_ps[:, :], w1_hi[:, k, :], lo[:, t.ring(PAIR), :], start=(k == 0), stop=False)
                    pe.matmul(h1_ps[:, :], w1_hi[:, k, :], hi[:, t.ring(PAIR), :], start=False, stop=False)
                    last = pe.matmul(h1_ps[:, :], w1_lo[:, k, :], hi[:, t.ring(PAIR), :], start=False, stop=(k == 1))
                last.then_inc(s_h1ps, 1)

            def layer2(t):
                if not there(t):
                    return
                pe.wait_ge(s_h1, t.g + 1)
                wait_count(pe, s_h2, t.g)
                pe.matmul(h2_ps[:, :], w2s[:, :], h1[:, t.ring(PAIR), :], start=True, stop=True).then_inc(s_h2ps, 1)

            def layer3(t):
                if not there(t):
                    return
                pe.wait_ge(s_h2, t.g + 1)
                pe.wait_ge(s_biased, t.g + 1)
                y = y_ps[t.ring(PAIR)]
                for r in range(ROWS):
                    last = pe.matmul(y[:, r * P:(r + 1) * P], h2[:, t.ring(PAIR), r * P:(r + 1) * P], w3c[:, :],
                                     start=False, stop=(r == ROWS - 1), skip_group_check=True)
                last.then_inc(s_yps, 1)

            def fast():
                keep_clock_up(14)
                turn_dst(0)
                keep_clock_up(6)

                def turn(at):
                    if is_first(at(0)):
                        wait_for_weights()
                        pe.wait_ge(s_rel, 3)
                        own_y_ps()
                    layer1(at(0))
                    if is_first(at(1)):
                        turn_dst(1)
                    turn_x(at(1))
                    if is_first(at(1)):
                        keep_clock_up(3)
                    sum_windows(at(1))
                    if is_first(at(1)):
                        keep_clock_up(6)
                    if is_last(at(0)):
                        layer3(at(-1))
                        layer2(at(0))
                    else:
                        layer2(at(0))
                        layer3(at(-1))
                all_turns(pe, turn)

            def general():
                wait_for_weights()
                own_y_ps()
                pe.sem_inc(s_gmm, GEN_EDGE_BUFS)

                def sum_all(t):
                    wait_count(pe, s_agglo, t.g)
                    pe.matmul(agg_ps[0][:, :], zeros[:, 0:P], zeros[:, :], start=True, stop=False)
                    with pe.Fori(0, GEN_BATCHES // GEN_EDGE_BUFS) as k:
                        for b in range(GEN_EDGE_BUFS):
                            nth = pe.snap(t.g * (GEN_BATCHES // GEN_EDGE_BUFS) + k)
                            pe.wait_ge(s_ge[b], (nth + 1) * 16)
                            pe.wait_ge(s_ghot, nth * GEN_EDGE_BUFS + b + 1)
                            for c in range(GEN_COLS):
                                last = pe.matmul(agg_ps[0][:, :], gen_edges[:, b, c, :], gen_hot[:, b % PAIR, c, :],
                                                 start=False, stop=False)
                            last.then_inc(s_gmm, 1)
                    pe.matmul(agg_ps[0][:, :], zeros[:, 0:P], zeros[:, :], start=False, stop=True) \
                        .then_inc(s_aggps, 1)

                def turn(t):
                    for stage in (turn_x, sum_all, layer1, layer2, layer3):
                        stage(t)
                general_turns(pe, turn)

            two_paths(pe, fast, general)


_INS = ["x", "dst", "edge_attr_128", "L0_gnn_W1", "L0_gnn_b1", "L0_gnn_W2", "L0_gnn_b2", "L0_gnn_W3", "L0_gnn_b3",
        "L0_gnn_ln_gamma", "L0_gnn_ln_beta"]


def kernel(**inputs):
    import numpy as _np
    import concourse.bacc as _bacc
    from concourse import mybir as _mybir
    from concourse.bass_utils import run_bass_kernel_spmd as _run

    nc = _bacc.Bacc("TRN2", target_bir_lowering=False, num_devices=1)
    arrays, args = {}, []
    for name in _INS:
        a = _np.ascontiguousarray(inputs[name])
        arrays[f"in_{name}_dram"] = a
        args.append(nc.dram_tensor(f"in_{name}_dram", a.shape, _mybir.dt.from_np(a.dtype), kind="ExternalInput").ap())
    shape = _np.shape(inputs["x"])
    args.append(nc.dram_tensor("out_0_dram", shape, _mybir.dt.from_np(_np.dtype("float32")),
                               kind="ExternalOutput").ap())
    gnn_layer(nc, *args)
    r = _run(nc, [arrays], core_ids=[0])
    return r.results[0]["out_0_dram"]
```
